# Optimizing a Trainium2 kernel written in Bass

```python
import numpy as np
import jax
import jax.numpy as jnp

def _softmax(x, axis=-1):
    return jax.nn.softmax(x, axis=axis)

def _gelu(x):
    return jax.nn.gelu(x, approximate=True)

def _silu(x):
    return jax.nn.silu(x)

def _sigmoid(x):
    return jax.nn.sigmoid(x)

def _layernorm(x, axis=-1, eps=1e-05):
    m = jnp.mean(x, axis=axis, keepdims=True)
    v = jnp.var(x, axis=axis, keepdims=True)
    return (x - m) / jnp.sqrt(v + eps)

def _scatter_add(tgt, idx, src, axis=0):
    return tgt.at[idx].add(src)

def _segment_sum(src, seg, n):
    return jax.ops.segment_sum(src, seg, n)
kernel_name = 'mk_adj_resnorm_d2_adj_r2_0e04cb'

def setup_inputs(seed: int=0):
    np.random.seed(seed)
    _w = jnp.asarray

    def _rec_inputs():
        import jax
        import jax.numpy as jnp
        _gk = jax.random.key(seed)
        x = -0.0002928 + 1 * jax.random.normal(jax.random.fold_in(_gk, 1), (64, 128, 256), jnp.float32)
        _w = (1.0 + jnp.arange(128, dtype=jnp.float32)) ** (-0.5)
        _w = _w / _w.mean()
        _pij = jnp.clip(0.0625 * _w[:, None] * _w[None, :], 0.0, 1.0)
        _a = jax.random.uniform(jax.random.fold_in(_gk, 2), (64, 128, 128)) < _pij
        _a = jnp.logical_or(_a, jnp.eye(128, dtype=bool))
        adj = _a.astype(jnp.int32)
        return (x, adj)
    x, adj = _rec_inputs()

    def _L0_gnn_setup():
        import jax, jax.numpy as jnp
        import numpy as np
        B, N, D = (8, 512, 256)
        NH = 8
        DK = D // NH
        key = jax.random.key(seed)
        ks = jax.random.split(key, 6)
        x = jax.random.normal(ks[0], (B, N, D), dtype=jnp.float32)
        adj = jax.random.randint(ks[1], (B, N, N), 0, 2, dtype=jnp.int32)
        adj = jnp.maximum(adj, jnp.eye(N, dtype=jnp.int32)[None])
        s = 1.0 / np.sqrt(D)
        Wq = jax.random.normal(ks[2], (D, D), dtype=jnp.float32) * s
        Wk = jax.random.normal(ks[3], (D, D), dtype=jnp.float32) * s
        Wv = jax.random.normal(ks[4], (D, D), dtype=jnp.float32) * s
        Wo = jax.random.normal(ks[5], (D, D), dtype=jnp.float32) * s
        return {'x': x, 'adj': adj, 'Wq': Wq, 'Wk': Wk, 'Wv': Wv, 'Wo': Wo}
    _L0_gnn_all = _L0_gnn_setup()
    _L0_gnn_in = {k: v for k, v in _L0_gnn_all.items() if k in ('Wq', 'Wk', 'Wv', 'Wo')}
    del _L0_gnn_all

    def _L1_gnn_setup():
        import jax, jax.numpy as jnp
        import numpy as np
        L = 3
        D = 256
        B, N = (8, 512)
        EPS = 1e-05

        def layernorm(x, gamma, beta):
            mu = jnp.mean(x, axis=-1, keepdims=True)
            var = jnp.var(x, axis=-1, keepdims=True)
            return (x - mu) * jax.lax.rsqrt(var + EPS) * gamma + beta
        key = jax.random.key(seed)
        ks = jax.random.split(key, 12)
        s = 1.0 / np.sqrt(D)
        node_features = jax.random.normal(ks[0], (B, N, D), dtype=jnp.float32)
        adjacency_matrix = jax.random.randint(ks[1], (B, N, N), 0, 2, dtype=jnp.int32)
        return {'node_features': node_features, 'adjacency_matrix': adjacency_matrix, 'attn_w': jax.random.normal(ks[2], (L, 2 * D), dtype=jnp.float32) * (1.0 / np.sqrt(2 * D)), 'attn_b': jax.random.normal(ks[3], (L,), dtype=jnp.float32) * 0.01, 'W1': jax.random.normal(ks[4], (L, D, 4 * D), dtype=jnp.float32) * s, 'b1': jnp.zeros((L, 4 * D), dtype=jnp.float32), 'W2': jax.random.normal(ks[5], (L, 4 * D, D), dtype=jnp.float32) * (1.0 / np.sqrt(4 * D)), 'b2': jnp.zeros((L, D), dtype=jnp.float32), 'g1': jnp.ones((L, D), dtype=jnp.float32), 'beta1': jnp.zeros((L, D), dtype=jnp.float32), 'g2': jnp.ones((L, D), dtype=jnp.float32), 'beta2': jnp.zeros((L, D), dtype=jnp.float32)}
    _L1_gnn_all = _L1_gnn_setup()
    _L1_gnn_in = {k: v for k, v in _L1_gnn_all.items() if k in ('attn_w', 'attn_b', 'W1', 'b1', 'W2', 'b2', 'g1', 'beta1', 'g2', 'beta2')}
    del _L1_gnn_all
    return {'x': x, 'adj': adj, 'L0_gnn_Wq': _L0_gnn_in['Wq'], 'L0_gnn_Wk': _L0_gnn_in['Wk'], 'L0_gnn_Wv': _L0_gnn_in['Wv'], 'L0_gnn_Wo': _L0_gnn_in['Wo'], 'L1_gnn_attn_w': _L1_gnn_in['attn_w'], 'L1_gnn_attn_b': _L1_gnn_in['attn_b'], 'L1_gnn_W1': _L1_gnn_in['W1'], 'L1_gnn_b1': _L1_gnn_in['b1'], 'L1_gnn_W2': _L1_gnn_in['W2'], 'L1_gnn_b2': _L1_gnn_in['b2'], 'L1_gnn_g1': _L1_gnn_in['g1'], 'L1_gnn_beta1': _L1_gnn_in['beta1'], 'L1_gnn_g2': _L1_gnn_in['g2'], 'L1_gnn_beta2': _L1_gnn_in['beta2']}

def reference(x, adj, L0_gnn_Wq, L0_gnn_Wk, L0_gnn_Wv, L0_gnn_Wo, L1_gnn_attn_w, L1_gnn_attn_b, L1_gnn_W1, L1_gnn_b1, L1_gnn_W2, L1_gnn_b2, L1_gnn_g1, L1_gnn_beta1, L1_gnn_g2, L1_gnn_beta2):
    import jax
    import jax.numpy as jnp

    def _L0_gnn_ref(x, adj, Wq, Wk, Wv, Wo):
        import jax, jax.numpy as jnp
        import numpy as np
        B, N, D = (8, 512, 256)
        NH = 8
        DK = D // NH
        b, n, d = x.shape
        sqrt_dk = jnp.asarray(np.sqrt(DK), dtype=x.dtype)

        def heads(t):
            return t.reshape(b, n, NH, DK).transpose(0, 2, 1, 3)
        q = heads(x @ Wq)
        k = heads(x @ Wk)
        v = heads(x @ Wv)
        scores = jnp.einsum('bhnd,bhmd->bhnm', q, k) / sqrt_dk
        mask = adj.astype(bool)[:, None]
        scores = jnp.where(mask, scores, -jnp.inf)
        attn = jax.nn.softmax(scores, axis=-1)
        out = jnp.einsum('bhnm,bhmd->bhnd', attn, v)
        out = out.transpose(0, 2, 1, 3).reshape(b, n, d)
        return jax.nn.relu(out) @ Wo

    def _L1_gnn_ref(node_features, adjacency_matrix, attn_w, attn_b, W1, b1, W2, b2, g1, beta1, g2, beta2):
        import jax, jax.numpy as jnp
        import numpy as np
        L = 3
        D = 256
        B, N = (8, 512)
        EPS = 1e-05

        def layernorm(x, gamma, beta):
            mu = jnp.mean(x, axis=-1, keepdims=True)
            var = jnp.var(x, axis=-1, keepdims=True)
            return (x - mu) * jax.lax.rsqrt(var + EPS) * gamma + beta
        n = adjacency_matrix.shape[-1]
        mask = adjacency_matrix.astype(jnp.float32) + jnp.eye(n, dtype=jnp.float32) > 0
        x = node_features
        d = x.shape[-1]
        for l in range(attn_w.shape[0]):
            si = x @ attn_w[l, :d]
            sj = x @ attn_w[l, d:]
            scores = si[:, :, None] + sj[:, None, :] + attn_b[l]
            scores = jnp.where(scores >= 0, scores, 0.2 * scores)
            scores = jnp.where(mask, scores, -jnp.inf)
            attn = jax.nn.softmax(scores, axis=-1)
            agg = jnp.einsum('bij,bjd->bid', attn, x)
            h = layernorm(x + agg, g1[l], beta1[l])
            ff = jax.nn.gelu(h @ W1[l] + b1[l], approximate=False) @ W2[l] + b2[l]
            x = layernorm(h + ff, g2[l], beta2[l])
        return x
    x = _layernorm(x + _L0_gnn_ref(x, adj, L0_gnn_Wq, L0_gnn_Wk, L0_gnn_Wv, L0_gnn_Wo), axis=-1)
    x = _layernorm(x + _L1_gnn_ref(x, adj, L1_gnn_attn_w, L1_gnn_attn_b, L1_gnn_W1, L1_gnn_b1, L1_gnn_W2, L1_gnn_b2, L1_gnn_g1, L1_gnn_beta1, L1_gnn_g2, L1_gnn_beta2), axis=-1)
    return x

_drawn_inputs = setup_inputs


def setup_inputs(seed=0):
    import zlib

    import numpy as np

    out = dict(_drawn_inputs(seed))
    spreads = {'L1_gnn_b1': (0.0, 0.1),
     'L1_gnn_b2': (0.0, 0.1),
     'L1_gnn_g1': (1.0, 0.2),
     'L1_gnn_beta1': (0.0, 0.1),
     'L1_gnn_g2': (1.0, 0.2),
     'L1_gnn_beta2': (0.0, 0.1)}
    factors = {'L1_gnn_attn_b': 64.0}
    for name, (base, spread) in spreads.items():
        noise = np.random.default_rng([zlib.crc32(name.encode()), seed]).standard_normal(out[name].shape)
        drawn = base * np.exp(spread * noise) if base else spread * noise
        out[name] = jnp.asarray(drawn.astype(out[name].dtype))
    for name, factor in factors.items():
        out[name] = (out[name] * factor).astype(out[name].dtype)
    return out
```

```python
from contextlib import ExitStack

import concourse.bass as bass
from concourse import mybir

F32 = mybir.dt.float32
F32R = mybir.dt.float32r
I32 = mybir.dt.int32
ALU = mybir.AluOpType
ACT = mybir.ActivationFunctionType
AX = mybir.AxisListType

P = 128
GROUP = 4
EPS = 1e-5
MASKED = -1e30
LOWEST = -3.0e38


def split_product(pe, out, w, x, w_of, x_of):
    terms = [(a, b, k) for k in range(2) for a, b in ((0, 0), (0, 1), (1, 0))]
    for n, (a, b, k) in enumerate(terms):
        last = pe.matmul(out, w_of(w[a], k), x_of(x[b], k), start=(n == 0), stop=(n == len(terms) - 1))
    return last


def gnn_kernel(nc, x_in, adj, Wq, Wk, Wv, Wo, attn_w, attn_b, W1, b1, W2, b2, g1, beta1, g2, beta2, out):
    B, N, D = x_in.shape
    L, F = b1.shape
    NH = 8
    DK = D // NH
    KT = D // P
    FT = F // P
    NG = B // GROUP
    TOK = GROUP * N
    T = L * NG
    SCALE = 1.0 / float(DK) ** 0.5
    assert N == P and KT == 2 and TOK == 512 and FT == 8 and NG % 2 == 0

    hist = nc.dram_tensor("hist", [T + NG, GROUP, N, D], F32).ap()
    mask_hist = nc.dram_tensor("mask_hist", [NG, GROUP, N, N], F32).ap()
    x_g = x_in.rearrange("(t j) p d -> t j p d", j=GROUP)
    adj_g = adj.rearrange("(t j) p m -> t j p m", j=GROUP)
    out_g = out.rearrange("(t j) p d -> t j p d", j=GROUP)

    def layer_of(t):
        l = t >> (NG.bit_length() - 1)
        return l if isinstance(l, int) else nc.s_assert_within(
            l, 0, L - 1, skip_runtime_bounds_check_because="t is a step, below L * NG")

    def block_of(dram, t):
        return dram[bass.ds(t, 1)].rearrange("o j p d -> p (o j) d")

    with ExitStack() as whole:
        def tensor_maker(ctx, stage=""):
            return lambda name, shape, dt=F32: ctx.enter_context(nc.sbuf_tensor(stage + name, shape, dt))

        def sem_maker(ctx):
            return lambda *names: [ctx.enter_context(nc.semaphore(n)) for n in names]

        sb, sems = tensor_maker(whole), sem_maker(whole)
        ps = whole.enter_context(nc.psum_tensor("ps", [P, 8, 512], F32))
        ident = sb("ident", [P, P])
        b1_cols = sb("b1_cols", [P, L, FT])
        affine = sb("affine", [P, L, 5, D])
        b2_rows = sb("b2_rows", [P, L, D])
        half_neg = sb("half_neg", [P, GROUP])
        w1_raw = sb("w1_raw", [P, KT, F])
        w2_raw = sb("w2_raw", [P, FT, D])
        ident_set, const_ld, w_ld, aff_set = sems("ident_set", "const_ld", "w_ld", "aff_set")
        stored = sems("stored_even", "stored_odd")

        def load_layer_weights(e, layer):
            e.dma_start(w1_raw[:], W1[bass.ds(layer, 1)].rearrange("o (k p) f -> p (o k) f", p=P)).then_inc(w_ld, 16)
            e.dma_start(w2_raw[:], W2[bass.ds(layer, 1)].rearrange("o (m p) d -> p (o m) d", p=P)).then_inc(w_ld, 16)

        fence_dve = sb("fence_dve", [P, 64])
        holds = {"dve": 0, "pool": 0}
        fence_pool = sb("fence_pool", [P, 64])

        def hold_dve(e, sem, value):
            e.wait_ge(sem, value)
            n = holds["dve"] = holds["dve"] + 1
            e.memset(fence_dve[:, n:n + 1], 0.0)

        def hold_pool(e, sem, value):
            e.wait_ge(sem, value)
            n = holds["pool"] = holds["pool"] + 1
            e.tensor_tensor(fence_pool[:, n:n + 1], half_neg[:, 0:1], half_neg[:, 0:1], ALU.add)

        def layernorm_on_pool(e, chain, n0, stats, inv, y, dest, done=None):
            e.tensor_scalar(inv[:, 0, :], stats[:, :, 1], EPS, None, ALU.add).then_inc(chain, 1)
            e.tensor_scalar(inv[:, 1, :], stats[:, :, 0], -1.0, None, ALU.mult).then_inc(chain, 1)
            e.wait_ge(chain, n0 + 1)
            e.tensor_tensor(inv[:, 2, :], inv[:, 0, :], half_neg[:], ALU.pow).then_inc(chain, 1)
            e.wait_ge(chain, n0 + 3)
            e.tensor_tensor(inv[:, 3, :], inv[:, 1, :], inv[:, 2, :], ALU.mult).then_inc(chain, 1)
            hold_pool(e, chain, n0 + 4)
            for j in range(GROUP):
                last = e.tensor_scalar(dest[:, j, :], y[:, j, 0:D], inv[:, 2, j:j + 1], inv[:, 3, j:j + 1],
                                       ALU.mult, ALU.add)
            last.then_inc(chain if done is None else done, 1)

        with ExitStack() as ctx:
            sb = tensor_maker(ctx, "att_")
            w_raw = sb("w_raw", [P, 4, KT, D])
            w_hi = sb("w_hi", [P, 4, KT, D], F32R)
            w_lo = sb("w_lo", [P, 4, KT, D], F32R)
            xl = [sb(f"xl{i}", [P, GROUP, D]) for i in range(2)]
            adjl = [sb(f"adjl{i}", [P, GROUP, N], I32) for i in range(2)]
            mask = [sb(f"mask{i}", [P, GROUP, N]) for i in range(2)]
            eye_sum = sb("eye_sum", [P, GROUP, N])
            mask1 = [sb(f"mask1_{i}", [P, GROUP, N]) for i in range(2)]
            xT = [sb("xT_hi", [P, KT, TOK], F32R), sb("xT_lo", [P, KT, TOK], F32R)]
            qk = [sb(f"qk{i}", [P, 4, TOK]) for i in range(2)]
            VW = DK + 2
            v = [sb(f"v{i}", [P, GROUP, NH, VW]) for i in range(2)]
            probs = sb("probs", [P, NH, N])
            probsT = sb("probsT", [P, NH, N])
            peak = sb("peak", [P, NH])
            neg_peak = sb("neg_peak", [P, NH])
            rden = sb("rden", [P, NH])
            att = sb("att", [P, D])
            attT = [sb("attT_hi", [P, KT, N], F32R), sb("attT_lo", [P, KT, N], F32R)]
            y = [sb(f"ya{i}", [P, GROUP, D]) for i in range(2)]
            stats = sb("a_stats", [P, GROUP, 6])
            mv = [sb(f"mv{i}", [P, GROUP, 2]) for i in range(2)]
            inv = sb("a_inv", [P, 4, GROUP])
            xo = [sb(f"xo{i}", [P, GROUP, D]) for i in range(2)]

            wa_ld, wa_split = sems("wa_ld", "wa_split")
            x_ld = sems("x_ld_even", "x_ld_odd")
            mask1_st = sems("mask1_st_even", "mask1_st_odd")
            (masks_made, v_set, xT_made, xT_hi_out, xT_lo_out, proj_made, proj_out, s_made, scored, peaked,
             exped, pT_made, pT_out_b, pT_out_a, pv_made, den_inv, att_out, attT_made, attT_hi_out,
             attT_lo_out, wo_made, y_out, bn_out, mv_out, ln_chain, ln_out, eye_made, eye_added) = sems(
                "masks_made", "v_set", "xT_made", "xT_hi_out", "xT_lo_out", "proj_made", "proj_out", "s_made",
                "scored", "peaked", "exped", "pT_made", "pT_out_b", "pT_out_a", "pv_made", "den_inv", "att_out",
                "attT_made", "attT_hi_out", "attT_lo_out", "wo_made", "y_out", "bn_out", "mv_out", "ln_chain",
                "ln_out", "eye_made", "eye_added")

            S = ps[:, 0:4, 0:2 * N]
            A = [ps[:, 4, :], ps[:, 5, :]]
            PB = [ps[:, 6, :], ps[:, 7, :]]

            def steps(e, body, tail=1):
                with e.Fori(0, NG // 2 - 1) as q:
                    for par in range(2):
                        body(q, par, True)
                body(NG // 2 - 1, 0, True)
                body(NG // 2 - 1, 1, False)

            block = ctx.enter_context(nc.Block())

            @block.sync
            def _(e):
                def load(t, par):
                    e.dma_start(xl[par][:], block_of(x_g, t)).then_inc(x_ld[par], 16)
                    e.dma_start(adjl[par][:], block_of(adj_g, t)).then_inc(x_ld[par], 16)

                for n, w in enumerate((Wq, Wk, Wv, Wo)):
                    e.dma_start(w_raw[:, n], w.rearrange("(k p) n -> p k n", p=P)).then_inc(wa_ld, 16)
                load(0, 0)
                load(1, 1)
                load_layer_weights(e, 0)

                def body(q, par, more):
                    t = 2 * q + par
                    e.wait_ge(masks_made, 2 * (t + 1))
                    e.dma_start(block_of(mask_hist, t), mask1[par][:]).then_inc(mask1_st[par], 16)
                    if more:
                        e.wait_ge(y_out, GROUP * (t + 1))
                        load(t + 2, par)
                    e.wait_ge(ln_out, t + 1)
                    e.dma_start(block_of(hist, t), xo[par][:]).then_inc(stored[par], 16)

                with e.Fori(0, NG // 2 - 1) as q:
                    for par in range(2):
                        body(q, par, True)
                body(NG // 2 - 1, 0, False)
                body(NG // 2 - 1, 1, False)
                for par in range(2):
                    e.wait_ge(mask1_st[par], 16 * (NG // 2))
                    e.wait_ge(stored[par], 16 * (NG // 2))

            @block.gpsimd
            def _(e):
                e.memset(ident[:], 0.0).then_inc(eye_made, 1)
                e.wait_ge(eye_made, 1)
                e.affine_select(out=ident[:], in_=ident[:], compare_op=ALU.not_equal, fill=1.0, base=0,
                                pattern=[[-1, P]], channel_multiplier=1).then_inc(ident_set, 1)
                e.memset(half_neg[:], -0.5).then_inc(eye_made, 1)
                for par in range(2):
                    e.memset(v[par][:], 1.0).then_inc(v_set, 1)
                e.wait_ge(const_ld, 16 * 6 * L)
                e.tensor_tensor(affine[:, :, 2, :], affine[:, :, 1, :], b2_rows[:], ALU.add).then_inc(aff_set, 1)
                e.wait_ge(eye_made, 2)

                def body(q, par, more):
                    t = 2 * q + par
                    e.wait_ge(stored[par], 16 * q)
                    hold_pool(e, mv_out, t + 1)
                    layernorm_on_pool(e, ln_chain, 4 * t, mv[par], inv, y[par], xo[par], ln_out)
                    e.wait_ge(ln_out, t + 1)

                steps(e, body)

            @block.tensor
            def _(e):
                e.wait_ge(ident_set, 1)
                e.wait_ge(wa_split, 2)

                def transposes(q1, par):
                    e.wait_ge(x_ld[par], 32 * (q1 + 1))
                    for k in range(KT):
                        for j in range(GROUP):
                            mm = e.transpose(A[k][:, j * N:(j + 1) * N], xl[par][:, j, k * P:(k + 1) * P], ident[:])
                        mm.then_inc(xT_made, 1)

                def project(t1, par, n):
                    bank = A[n % 2]
                    if n == 0:
                        e.wait_ge(xT_hi_out, 2 * (t1 + 1))
                        e.wait_ge(xT_lo_out, 2 * (t1 + 1))
                    if n >= 2:
                        e.wait_ge(proj_out, 6 * t1 + n - 1)
                    if n < 4:
                        mm = split_product(e, bank, (w_hi, w_lo), xT,
                                           lambda w, k: w[:, n // 2, k, (n % 2) * P:(n % 2 + 1) * P],
                                           lambda x, k: x[:, k, :])
                    else:
                        for h in range(2):
                            j = 2 * (n - 4) + h
                            mm = split_product(e, bank[:, h * D:(h + 1) * D], xT, (w_hi, w_lo),
                                               lambda x, k: x[:, k, j * N:(j + 1) * N],
                                               lambda w, k: w[:, 2, k, :])
                    mm.then_inc(proj_made, 1)

                def scores(par, j):
                    for h in range(NH):
                        r, c = h % 4, h // 4
                        rows = slice(DK * r, DK * (r + 1))
                        mm = e.matmul(S[:, r, c * N:(c + 1) * N], qk[par][rows, c, j * N:(j + 1) * N],
                                      qk[par][rows, 2 + c, j * N:(j + 1) * N], start=True, stop=True)
                    mm.then_inc(s_made, 1)

                def body(q, par, more):
                    t = 2 * q + par
                    for j in range(GROUP):
                        i = GROUP * t + j
                        e.wait_ge(exped, 2 * i + 1)
                        for h in range(4, 8):
                            mm = e.transpose(PB[1][:, (h - 4) * N:(h - 3) * N], probs[:, h, :], ident[:])
                        mm.then_inc(pT_made, 1)
                        e.wait_ge(exped, 2 * i + 2)
                        e.wait_ge(y_out, i)
                        for h in range(4):
                            mm = e.transpose(PB[0][:, h * N:(h + 1) * N], probs[:, h, :], ident[:])
                        mm.then_inc(pT_made, 1)
                        if j < GROUP - 1:
                            scores(par, j + 1)
                        elif more:
                            e.wait_ge(proj_out, 6 * (t + 1) + 4)
                            scores(1 - par, 0)
                        e.wait_ge(pT_out_a, i + 1)
                        e.wait_ge(pT_out_b, i + 1)
                        if j == 0:
                            e.wait_ge(proj_out, 6 * (t + 1))
                        for h in range(NH):
                            mm = e.matmul(PB[0][:, h * VW:(h + 1) * VW], probsT[:, h, :], v[par][:, j, h, :],
                                          start=True, stop=True)
                        mm.then_inc(pv_made, 1)
                        if more and j == 1:
                            transposes(q + (par + 1) // 2, 1 - par)
                        if more and j == 2:
                            project(t + 1, 1 - par, 0)
                            project(t + 1, 1 - par, 1)
                        if more and j == 3:
                            project(t + 1, 1 - par, 4)
                        e.wait_ge(att_out, i + 1)
                        for k in range(KT):
                            mm = e.transpose(PB[1][:, k * N:(k + 1) * N], att[:, k * P:(k + 1) * P], ident[:])
                        mm.then_inc(attT_made, 1)
                        if more and j == 2:
                            project(t + 1, 1 - par, 2)
                            project(t + 1, 1 - par, 3)
                        if more and j == 3:
                            project(t + 1, 1 - par, 5)
                        e.wait_ge(attT_hi_out, i + 1)
                        e.wait_ge(attT_lo_out, i + 1)
                        split_product(e, PB[0][:, 0:D], attT, (w_hi, w_lo), lambda x, k: x[:, k, :],
                                      lambda w, k: w[:, 3, k, :]).then_inc(wo_made, 1)

                transposes(0, 0)
                for n in range(4):
                    project(0, 0, n)
                e.wait_ge(proj_out, 4)
                scores(0, 0)
                project(0, 0, 4)
                project(0, 0, 5)
                steps(e, body)

            @block.scalar
            def _(e):
                with nc.allow_non_contiguous_dma(reason="columns of b1, once"):
                    for l in range(L):
                        e.dma_start(b1_cols[:, l, :], b1[l].rearrange("(m p) -> p m", p=P)).then_inc(const_ld, 16)
                for l in range(L):
                    for n, c in ((0, g1), (1, beta1), (3, g2), (4, beta2)):
                        e.dma_start(affine[:, l, n, :], c[l:l + 1, :].to_broadcast([P, D])).then_inc(const_ld, 16)
                    e.dma_start(b2_rows[:, l, :], b2[l:l + 1, :].to_broadcast([P, D])).then_inc(const_ld, 16)

                def xT_hi(t1):
                    for k in range(KT):
                        e.wait_ge(xT_made, 2 * t1 + k + 1)
                        e.copy(xT[0][:, k, :], A[k]).then_inc(xT_hi_out, 1)

                def proj_copy(t1, par, n):
                    e.wait_ge(proj_made, 6 * t1 + n + 1)
                    if n < 4:
                        e.copy(qk[par][:, n, :], A[n % 2]).then_inc(proj_out, 1)
                    else:
                        for h in range(2):
                            ins = e.copy(v[par][:, 2 * (n - 4) + h, :, 0:DK],
                                         A[n % 2][:, h * D:(h + 1) * D].rearrange("p (h d) -> p h d", d=DK))
                        ins.then_inc(proj_out, 1)

                def exps(i, half):
                    for h in range(4 - 4 * half, 8 - 4 * half):
                        ins = e.activation(probs[:, h, :], probs[:, h, :], ACT.Exp, bias=neg_peak[:, h:h + 1], scale=SCALE)
                    ins.then_inc(exped, 1)

                def body(q, par, more):
                    t = 2 * q + par
                    for j in range(GROUP):
                        i = GROUP * t + j
                        e.wait_ge(pT_made, 2 * i + 1)
                        e.copy(probsT[:, 4:8, :].rearrange("p h n -> p (h n)"), PB[1]).then_inc(pT_out_b, 1)
                        if more and j == 1:
                            xT_hi(t + 1)
                        if more and j == 2:
                            proj_copy(t + 1, 1 - par, 0)
                            proj_copy(t + 1, 1 - par, 1)
                        if more and j == 3:
                            proj_copy(t + 1, 1 - par, 4)
                        if more or j < GROUP - 1:
                            e.wait_ge(peaked, i + 2)
                            exps(i + 1, 0)
                        e.wait_ge(attT_made, i + 1)
                        e.copy(attT[0][:].rearrange("p k n -> p (k n)"), PB[1][:, 0:D]).then_inc(attT_hi_out, 1)
                        if more or j < GROUP - 1:
                            exps(i + 1, 1)
                        if more and j == 2:
                            proj_copy(t + 1, 1 - par, 2)
                            proj_copy(t + 1, 1 - par, 3)
                        if more and j == 3:
                            proj_copy(t + 1, 1 - par, 5)

                xT_hi(0)
                for n in range(4):
                    proj_copy(0, 0, n)
                e.wait_ge(v_set, 2)
                e.wait_ge(peaked, 1)
                exps(0, 0)
                exps(0, 1)
                proj_copy(0, 0, 4)
                proj_copy(0, 0, 5)
                steps(e, body)

            @block.vector
            def _(e):
                e.wait_ge(wa_ld, 64)
                e.tensor_copy(w_hi[:], w_raw[:]).then_inc(wa_split, 1)
                e.wait_ge(wa_split, 1)
                e.tensor_tensor(w_lo[:], w_raw[:], w_hi[:].bitcast(F32), ALU.subtract).then_inc(wa_split, 1)
                e.wait_ge(ident_set, 1)

                def make_masks(q1, par, t1, first=False):
                    e.wait_ge(x_ld[par], 32 * (q1 + 1))
                    e.tensor_scalar(mask[par][:], adjl[par][:], 0.0, MASKED, ALU.is_equal, ALU.mult).then_inc(masks_made, 1)
                    for j in range(GROUP):
                        ins = e.tensor_tensor(eye_sum[:, j, :], adjl[par][:, j, :], ident[:], ALU.add)
                    ins.then_inc(eye_added, 1)
                    e.wait_ge(eye_added, t1 + 1)
                    if not first:
                        e.wait_ge(mask1_st[par], 16 * q1)
                    e.tensor_scalar(mask1[par][:], eye_sum[:], 0.0, MASKED, ALU.is_le, ALU.mult).then_inc(masks_made, 1)

                def xT_lo(t1):
                    for k in range(KT):
                        e.wait_ge(xT_hi_out, 2 * t1 + k + 1)
                        e.tensor_tensor(xT[1][:, k, :], A[k], xT[0][:, k, :].bitcast(F32), ALU.subtract).then_inc(xT_lo_out, 1)

                def masked_scores(i, t_, par, j):
                    e.wait_ge(s_made, i + 1)
                    hold_dve(e, masks_made, 2 * t_ + 1)
                    for h in range(NH):
                        r, c = h % 4, h // 4
                        ins = e.tensor_tensor_reduce(out=probs[:, h, :], in0=S[:, r, c * N:(c + 1) * N],
                                                     in1=mask[par][:, j, :], scale=1.0, scalar=LOWEST,
                                                     op0=ALU.add, op1=ALU.max, accum_out=peak[:, h:h + 1])
                    ins.then_inc(scored, 1)
                    e.wait_ge(scored, i + 1)
                    e.tensor_scalar(neg_peak[:], peak[:], -SCALE, None, ALU.mult).then_inc(peaked, 1)

                def body(q, par, more):
                    t = 2 * q + par
                    for j in range(GROUP):
                        i = GROUP * t + j
                        e.wait_ge(pT_made, 2 * i + 2)
                        e.tensor_copy(probsT[:, 0:4, :].rearrange("p h n -> p (h n)"), PB[0]).then_inc(pT_out_a, 1)
                        if more and j == 2:
                            make_masks(q + (par + 1) // 2, 1 - par, t + 1)
                        if more and j == 1:
                            xT_lo(t + 1)
                        if j < GROUP - 1:
                            masked_scores(i + 1, t, par, j + 1)
                        elif more:
                            masked_scores(i + 1, t + 1, 1 - par, 0)
                        e.wait_ge(pv_made, i + 1)
                        pv = PB[0][:, 0:NH * VW].rearrange("p (h w) -> p h w", w=VW)
                        e.reciprocal(rden[:], pv[:, :, DK]).then_inc(den_inv, 1)
                        e.wait_ge(den_inv, i + 1)
                        e.scalar_tensor_tensor(out=att[:].rearrange("p (h d) -> p h d", d=DK), in0=pv[:, :, 0:DK],
                                               scalar=0.0, in1=rden[:].rearrange("p (h o) -> p h o", o=1).to_broadcast([P, NH, DK]),
                                               op0=ALU.max, op1=ALU.mult).then_inc(att_out, 1)
                        e.wait_ge(attT_hi_out, i + 1)
                        e.tensor_tensor(attT[1][:].rearrange("p k n -> p (k n)"), PB[1][:, 0:D],
                                        attT[0][:].rearrange("p k n -> p (k n)").bitcast(F32),
                                        ALU.subtract).then_inc(attT_lo_out, 1)
                        if j == 0:
                            e.wait_ge(ln_out, 2 * q)
                        e.wait_ge(wo_made, i + 1)
                        e.tensor_tensor(y[par][:, j, :], PB[0][:, 0:D], xl[par][:, j, :], ALU.add).then_inc(y_out, 1)
                        e.wait_ge(y_out, i + 1)
                        e.bn_stats(stats[:, j, :], y[par][:, j, :]).then_inc(bn_out, 1)
                    hold_dve(e, bn_out, GROUP * (t + 1))
                    for j in range(GROUP):
                        ins = e.bn_aggr(mv[par][:, j, :], stats[:, j, :])
                    ins.then_inc(mv_out, 1)

                make_masks(0, 0, 0, True)
                xT_lo(0)
                masked_scores(0, 0, 0, 0)
                steps(e, body)

        with ExitStack() as ctx:
            sb = tensor_maker(ctx, "gnn_")
            W = [sb("w1_hi", [P, KT, F], F32R), sb("w1_lo", [P, KT, F], F32R)]
            V = [sb("w2_hi", [P, FT, D], F32R), sb("w2_lo", [P, FT, D], F32R)]
            XW = D + 2
            x = [sb(f"x{i}", [P, GROUP, XW]) for i in range(2)]
            mask = [sb(f"gmask{i}", [P, GROUP, N]) for i in range(2)]
            aw = [sb(f"aw{i}", [P, 2, D]) for i in range(2)]
            ab = [sb(f"ab{i}", [P, 1]) for i in range(2)]
            junk = sb("junk", [P, GROUP, 2, D])
            s_i = sb("s_i", [P, GROUP])
            s_j = sb("s_j", [P, GROUP])
            u = sb("u", [P, GROUP, N])
            top = sb("top", [P, GROUP])
            small = sb("small", [P, 5, GROUP])
            e1 = sb("e1", [P, GROUP, N])
            e2 = sb("e2", [P, GROUP, N])
            pT = sb("pT", [P, GROUP, N])
            rden = sb("grden", [P, GROUP])
            y1 = sb("res1", [P, GROUP, D])
            y2 = sb("res2", [P, GROUP, D])
            norm = sb("norm", [P, GROUP, D])
            h = sb("h", [P, GROUP, D])
            hb = [sb(f"hb{i}", [P, GROUP, D]) for i in range(2)]
            hT = [sb("hT_hi", [P, KT, TOK], F32R), sb("hT_lo", [P, KT, TOK], F32R)]
            g = [sb("g_hi", [P, FT, TOK], F32R), sb("g_lo", [P, FT, TOK], F32R)]
            st1 = sb("st1", [P, GROUP, 6])
            st2 = sb("st2", [P, GROUP, 6])
            mv1 = sb("mv1", [P, GROUP, 2])
            mv2 = sb("mv2", [P, GROUP, 2])
            inv = sb("ginv", [P, 4, GROUP])
            xo = [sb(f"gxo{i}", [P, GROUP, D]) for i in range(2)]

            g_ld = sems("g_ld_even", "g_ld_odd")
            (w_hi_set, w_split, x_ones, ff1_made, gelu_out, g_lo_out, pT_made, pT_out, agg_made, aij_out, sjT_made,
             u_out, bias_step, bias_out, exp_out, p_out, recip_out, y1_out, bn1_out, mv1_out, ln1, h_out, hb_out,
             hT_made, hT_hi_out, hT_lo_out, ff2_made, y2_out, bn2_out, mv2_out, ln2, norm2_out, x_out) = sems(
                *("g_" + n for n in (
                    "w_hi_set", "w_split", "x_ones", "ff1_made", "gelu_out", "g_lo_out", "pT_made", "pT_out",
                    "agg_made", "aij_out", "sjT_made", "u_out", "bias_step", "bias_out", "exp_out", "p_out",
                    "recip_out", "y1_out", "bn1_out", "mv1_out", "ln1", "h_out", "hb_out", "hT_made", "hT_hi_out",
                    "hT_lo_out", "ff2_made", "y2_out", "bn2_out", "mv2_out", "ln2", "norm2_out", "x_out")))

            FF1 = [ps[:, i, :] for i in range(3)]
            FF2 = [ps[:, 3, 0:D], ps[:, 4, 0:D]]
            AGG = [ps[:, 5, :], ps[:, 6, :]]
            TB = ps[:, 7, :]
            HT = [TB, AGG[0]]

            def steps(e, new_layer, body):
                pairs = NG // 2
                with e.Fori(0, L - 1) as l:
                    new_layer(l, True)
                    with e.Fori(0, pairs) as p:
                        for par in range(2):
                            body(l * pairs + p, par, True, True)
                new_layer(L - 1, False)
                with e.Fori((L - 1) * pairs, L * pairs - 1) as q:
                    for par in range(2):
                        body(q, par, True, True)
                body(L * pairs - 1, 0, True, False)
                body(L * pairs - 1, 1, False, False)

            def ahead(q, par, d):
                return 2 * q + (par + d), (par + d) % 2, q + (par + d) // 2

            block = ctx.enter_context(nc.Block())

            @block.sync
            def _(e):
                def load(t, par, half):
                    e.wait_ge(stored[par], 16 * (half + 1))
                    e.dma_start(x[par][:, :, 0:D], block_of(hist, t)).then_inc(g_ld[par], 16)
                    e.dma_start(mask[par][:], block_of(mask_hist, t & (NG - 1))).then_inc(g_ld[par], 16)
                    l = layer_of(t)
                    e.dma_start(aw[par][:].rearrange("p a d -> p (a d)"),
                                attn_w[bass.ds(l, 1), :].to_broadcast([P, 2 * D])).then_inc(g_ld[par], 16)
                    e.dma_start(ab[par][:], attn_b[bass.ds(l, 1)].rearrange("(a o) -> a o", o=1).to_broadcast([P, 1])).then_inc(g_ld[par], 16)

                def body(q, par, more=True):
                    t = 2 * q + par
                    if more:
                        t1, p1, h1 = ahead(q, par, 1)
                        t3, p3, h3 = ahead(q, par, 3)
                        e.wait_ge(y1_out, GROUP * (t1 + 1))
                        load(t3, p3, h3)
                    e.wait_ge(x_out, t + 1)
                    e.dma_start(block_of(hist, t + NG), xo[par][:]).then_inc(stored[par], 16)

                for t in range(2):
                    load(t, t, 0)
                e.wait_ge(y1_out, GROUP)
                load(2, 0, 1)
                pairs = NG // 2
                with e.Fori(0, L - 1) as l:
                    e.wait_ge(w_split, 2 * (l + 1))
                    load_layer_weights(e, l + 1)
                    with e.Fori(0, pairs) as p:
                        for par in range(2):
                            body(l * pairs + p, par)
                with e.Fori((L - 1) * pairs, L * pairs - 2) as q:
                    for par in range(2):
                        body(q, par)
                body(L * pairs - 2, 0)
                body(L * pairs - 2, 1, False)
                body(L * pairs - 1, 0, False)
                body(L * pairs - 1, 1, False)
                for par in range(2):
                    e.wait_ge(stored[par], 16 * (T + NG) // 2)

            @block.gpsimd
            def _(e):
                for par in range(2):
                    e.memset(x[par][:, :, D:XW], 1.0).then_inc(x_ones, 1)
                e.wait_ge(aff_set, 1)

                def row(l, n):
                    return affine[:, bass.ds(l, 1), n, :].to_broadcast([P, GROUP, D])

                def ln_attention(t1, par1):
                    l = layer_of(t1)
                    hold_pool(e, mv1_out, t1 + 1)
                    layernorm_on_pool(e, ln1, 6 * t1, mv1, inv, y1, norm)
                    e.wait_ge(ln1, 6 * t1 + 5)
                    e.tensor_tensor(norm[:], norm[:], row(l, 0), ALU.mult).then_inc(ln1, 1)
                    e.wait_ge(ln1, 6 * t1 + 6)
                    e.wait_ge(hT_made, 2 * t1)
                    e.tensor_tensor(h[:], norm[:], row(l, 1), ALU.add).then_inc(h_out, 1)
                    e.tensor_tensor(hb[par1][:], norm[:], row(l, 2), ALU.add).then_inc(hb_out, 1)
                    e.wait_ge(hb_out, t1 + 1)

                def ln_ffn(t, par, half):
                    l = layer_of(t)
                    hold_pool(e, mv2_out, t + 1)
                    layernorm_on_pool(e, ln2, 5 * t, mv2, inv, y2, norm, norm2_out)
                    e.wait_ge(norm2_out, t + 1)
                    e.tensor_tensor(norm[:], norm[:], row(l, 3), ALU.mult).then_inc(ln2, 1)
                    e.wait_ge(ln2, 5 * t + 5)
                    e.wait_ge(stored[par], 16 * (half + NG // 2))
                    e.tensor_tensor(xo[par][:], norm[:], row(l, 4), ALU.add).then_inc(x_out, 1)
                    e.wait_ge(x_out, t + 1)

                def body(q, par, a1, a2):
                    if a1:
                        t1, p1, _ = ahead(q, par, 1)
                        ln_attention(t1, p1)
                    ln_ffn(2 * q + par, par, q)

                ln_attention(0, 0)
                steps(e, lambda l, more: None, body)

            @block.tensor
            def _(e):
                def probs_T(t1):
                    e.wait_ge(p_out, t1 + 1)
                    for j in range(GROUP):
                        mm = e.transpose(TB[:, j * N:(j + 1) * N], e1[:, j, :], ident[:])
                    mm.then_inc(pT_made, 1)

                def aggregate(t1, par1):
                    e.wait_ge(pT_out, t1 + 1)
                    for j in range(GROUP):
                        if j >= 2:
                            e.wait_ge(y1_out, GROUP * t1 + j - 1)
                        e.matmul(AGG[j % 2][:, 0:XW], pT[:, j, :], x[par1][:, j, :], start=True, stop=True).then_inc(agg_made, 1)

                def spread_sj(t2):
                    e.wait_ge(aij_out, t2 + 1)
                    for j in range(GROUP):
                        mm = e.transpose(TB[:, j * N:(j + 1) * N], s_j[:, j:j + 1].to_broadcast([P, N]), ident[:])
                    mm.then_inc(sjT_made, 1)

                def transpose_h(t1):
                    e.wait_ge(h_out, t1 + 1)
                    for k in range(KT):
                        for j in range(GROUP):
                            mm = e.transpose(HT[k][:, j * N:(j + 1) * N], h[:, j, k * P:(k + 1) * P], ident[:])
                        mm.then_inc(hT_made, 1)

                def ffn2(t, j):
                    e.wait_ge(y2_out, GROUP * t + (j - 1 if j >= 2 else 0))
                    terms = [(m, a, b) for m in range(FT) for a, b in ((0, 0), (0, 1), (1, 0))]
                    for n, (m, a, b) in enumerate(terms):
                        mm = e.matmul(FF2[j % 2], g[a][:, m, j * N:(j + 1) * N], V[b][:, m, :],
                                      start=(n == 0), stop=(n == len(terms) - 1))
                    mm.then_inc(ff2_made, 1)

                def body(q, par, a1, a2):
                    t = 2 * q + par
                    t1, p1, _ = ahead(q, par, 1)
                    e.wait_ge(hT_hi_out, 2 * (t + 1))
                    e.wait_ge(hT_lo_out, 2 * (t + 1))
                    e.wait_ge(w_split, 2 * (layer_of(t) + 1))
                    for m in range(FT):
                        if m >= 3:
                            e.wait_ge(g_lo_out, FT * t + m - 2)
                        split_product(e, FF1[FFB[m]], W, hT, lambda w, k: w[:, k, m * P:(m + 1) * P],
                                      lambda x_, k: x_[:, k, :]).then_inc(ff1_made, 1)
                        if m == 3 and a1:
                            probs_T(t1)
                        if m == 5 and a1:
                            aggregate(t1, p1)
                    if a2:
                        spread_sj(t + 2)
                    e.wait_ge(g_lo_out, FT * (t + 1))
                    for j in range(GROUP):
                        if j == 3 and a1:
                            if a2:
                                e.wait_ge(u_out, t + 3)
                            transpose_h(t1)
                        ffn2(t, j)

                e.wait_ge(x_ones, 2)
                spread_sj(0)
                probs_T(0)
                aggregate(0, 0)
                spread_sj(1)
                e.wait_ge(u_out, 2)
                transpose_h(0)

                steps(e, lambda l, more: None, body)

            @block.scalar
            def _(e):
                def copy_pT(t1):
                    e.wait_ge(pT_made, t1 + 1)
                    e.copy(pT[:].rearrange("p j n -> p (j n)"), TB).then_inc(pT_out, 1)

                def exps(t2):
                    e.wait_ge(bias_out, t2 + 1)
                    for j in range(GROUP):
                        e.activation(e1[:, j, :], u[:, j, :], ACT.Exp, bias=small[:, 3, j:j + 1])
                        ins = e.activation(e2[:, j, :], u[:, j, :], ACT.Exp, bias=small[:, 4, j:j + 1], scale=0.2)
                    ins.then_inc(exp_out, 1)

                def hT_hi(t1):
                    for k in range(KT):
                        e.wait_ge(hT_made, 2 * t1 + k + 1)
                        e.copy(hT[0][:, k, :], HT[k]).then_inc(hT_hi_out, 1)

                def body(q, par, a1, a2):
                    t = 2 * q + par
                    l = layer_of(t)
                    for m in range(FT):
                        e.wait_ge(ff1_made, 8 * t + m + 1)
                        bias = b1_cols[:, bass.ds(l, 1), m]
                        e.activation(g[0][:, m, :], FF1[FFB[m]], ACT.Gelu, bias=bias)
                        e.activation(FF1[FFB[m]], FF1[FFB[m]], ACT.Gelu, bias=bias).then_inc(gelu_out, 1)
                        if m == 3 and a1:
                            copy_pT(t + 1)
                    if a2:
                        exps(t + 2)
                    if a1:
                        hT_hi(t + 1)

                exps(0)
                copy_pT(0)
                exps(1)
                hT_hi(0)
                steps(e, lambda l, more: None, body)

            @block.vector
            def _(e):
                def attention_sums(t2, par2, half2, j):
                    if j == 0:
                        e.wait_ge(g_ld[par2], 64 * (half2 + 1))
                    for n, s in ((0, s_i), (1, s_j)):
                        ins = e.tensor_tensor_reduce(out=junk[:, j, n, :], in0=x[par2][:, j, 0:D], in1=aw[par2][:, n, :],
                                                     scale=1.0, scalar=0.0, op0=ALU.mult, op1=ALU.add,
                                                     accum_out=s[:, j:j + 1])
                    if j == GROUP - 1:
                        ins.then_inc(aij_out, 1)

                def masked_sums(t2, par2):
                    hold_dve(e, sjT_made, t2 + 1)
                    for j in range(GROUP):
                        ins = e.tensor_tensor_reduce(out=u[:, j, :], in0=TB[:, j * N:(j + 1) * N], in1=mask[par2][:, j, :],
                                                     scale=1.0, scalar=LOWEST, op0=ALU.add, op1=ALU.max,
                                                     accum_out=top[:, j:j + 1])
                    ins.then_inc(u_out, 1)
                    e.wait_ge(aij_out, t2 + 1)
                    e.tensor_scalar(small[:, 0, :], s_i[:], ab[par2][:, 0:1], None, ALU.add).then_inc(bias_step, 1)
                    e.wait_ge(bias_step, 3 * t2 + 1)
                    e.wait_ge(u_out, t2 + 1)
                    e.tensor_tensor(small[:, 1, :], top[:], small[:, 0, :], ALU.add).then_inc(bias_step, 1)
                    e.wait_ge(bias_step, 3 * t2 + 2)
                    e.scalar_tensor_tensor(out=small[:, 2, :], in0=small[:, 1, :], scalar=0.2, in1=small[:, 1, :],
                                           op0=ALU.mult, op1=ALU.max).then_inc(bias_step, 1)
                    e.wait_ge(bias_step, 3 * t2 + 3)
                    e.tensor_tensor(small[:, 3, :], small[:, 0, :], small[:, 2, :], ALU.subtract)
                    e.scalar_tensor_tensor(out=small[:, 4, :], in0=small[:, 0, :], scalar=0.2, in1=small[:, 2, :],
                                           op0=ALU.mult, op1=ALU.subtract).then_inc(bias_out, 1)

                def probs_max(t1):
                    e.wait_ge(exp_out, t1 + 1)
                    e.tensor_tensor(e1[:], e1[:], e2[:], ALU.max).then_inc(p_out, 1)

                def residual1(t1, par1, j):
                    n = GROUP * t1 + j
                    bank = AGG[j % 2]
                    e.wait_ge(agg_made, n + 1)
                    e.reciprocal(rden[:, j:j + 1], bank[:, D:D + 1]).then_inc(recip_out, 1)
                    e.wait_ge(recip_out, n + 1)
                    e.scalar_tensor_tensor(out=y1[:, j, :], in0=bank[:, 0:D], scalar=rden[:, j:j + 1],
                                           in1=x[par1][:, j, 0:D], op0=ALU.mult, op1=ALU.add).then_inc(y1_out, 1)

                def stats1(t1, j):
                    e.wait_ge(y1_out, GROUP * t1 + j + 1)
                    e.bn_stats(st1[:, j, :], y1[:, j, :]).then_inc(bn1_out, 1)

                def attention_out(t1, par1):
                    e.wait_ge(h_out, t1)
                    residual1(t1, par1, 0)
                    residual1(t1, par1, 1)
                    stats1(t1, 0)
                    residual1(t1, par1, 2)
                    stats1(t1, 1)
                    residual1(t1, par1, 3)
                    stats1(t1, 2)
                    stats1(t1, 3)
                    hold_dve(e, bn1_out, GROUP * (t1 + 1))
                    for j in range(GROUP):
                        ins = e.bn_aggr(mv1[:, j, :], st1[:, j, :])
                    ins.then_inc(mv1_out, 1)

                def residual2(t, par, j):
                    n = GROUP * t + j
                    if j == 0:
                        e.wait_ge(hb_out, t + 1)
                        e.wait_ge(norm2_out, t)
                    e.wait_ge(ff2_made, n + 1)
                    e.tensor_tensor(y2[:, j, :], FF2[j % 2], hb[par][:, j, :], ALU.add).then_inc(y2_out, 1)

                def stats2(t, j):
                    e.wait_ge(y2_out, GROUP * t + j + 1)
                    e.bn_stats(st2[:, j, :], y2[:, j, :]).then_inc(bn2_out, 1)

                def gelu_lo(t, m):
                    e.wait_ge(gelu_out, 8 * t + m + 1)
                    e.tensor_tensor(g[1][:, m, :], FF1[FFB[m]], g[0][:, m, :].bitcast(F32), ALU.subtract).then_inc(g_lo_out, 1)

                def hT_lo(t1):
                    for k in range(KT):
                        e.wait_ge(hT_hi_out, 2 * t1 + k + 1)
                        e.tensor_tensor(hT[1][:, k, :], HT[k], hT[0][:, k, :].bitcast(F32), ALU.subtract).then_inc(hT_lo_out, 1)

                def body(q, par, a1, a2):
                    t = 2 * q + par
                    t1, p1, _ = ahead(q, par, 1)
                    t2, p2, h2 = ahead(q, par, 2)
                    if a1:
                        probs_max(t1)
                    for m in range(6):
                        gelu_lo(t, m)
                        if m < GROUP and a2:
                            attention_sums(t2, p2, h2, m)
                    if a1:
                        attention_out(t1, p1)
                    gelu_lo(t, 6)
                    gelu_lo(t, 7)
                    if a2:
                        masked_sums(t2, p2)
                    residual2(t, par, 0)
                    residual2(t, par, 1)
                    stats2(t, 0)
                    residual2(t, par, 2)
                    stats2(t, 1)
                    if a1:
                        hT_lo(t1)
                    stats2(t, 2)
                    residual2(t, par, 3)
                    stats2(t, 3)
                    hold_dve(e, bn2_out, GROUP * (t + 1))
                    for j in range(GROUP):
                        ins = e.bn_aggr(mv2[:, j, :], st2[:, j, :])
                    ins.then_inc(mv2_out, 1)

                def new_layer(l, more):
                    e.wait_ge(w_ld, 32 * (l + 1))
                    e.tensor_copy(W[0][:], w1_raw[:]).then_inc(w_hi_set, 1)
                    e.tensor_copy(V[0][:], w2_raw[:]).then_inc(w_hi_set, 1)
                    e.wait_ge(w_hi_set, 2 * l + 1)
                    e.tensor_tensor(W[1][:], w1_raw[:], W[0][:].bitcast(F32), ALU.subtract).then_inc(w_split, 1)
                    e.wait_ge(w_hi_set, 2 * l + 2)
                    e.tensor_tensor(V[1][:], w2_raw[:], V[0][:].bitcast(F32), ALU.subtract).then_inc(w_split, 1)

                for j in range(GROUP):
                    attention_sums(0, 0, 0, j)
                masked_sums(0, 0)
                probs_max(0)
                attention_out(0, 0)
                for j in range(GROUP):
                    attention_sums(1, 1, 0, j)
                masked_sums(1, 1)
                hT_lo(0)
                steps(e, new_layer, body)

        with ExitStack() as ctx:
            sb = tensor_maker(ctx, "fin_")
            NB = 4
            xa = [sb(f"xa{i}", [P, GROUP, D]) for i in range(NB)]
            xb = [sb(f"xb{i}", [P, GROUP, D]) for i in range(NB)]
            res = [sb(f"res{i}", [P, GROUP, D]) for i in range(NB)]
            st = [sb(f"fst{i}", [P, GROUP, 6]) for i in range(2)]
            mv = [sb(f"fmv{i}", [P, GROUP, 2]) for i in range(2)]
            inv = sb("finv", [P, 4, GROUP])
            ld = sems(*(f"f_ld{i}" for i in range(NB)))
            written = sems(*(f"f_written{i}" for i in range(NB)))
            sum_out, bn_out, mv_out, chain, fin = sems("f_sum", "f_bn", "f_mv", "f_chain", "f_fin")
            block = ctx.enter_context(nc.Block())

            @block.sync
            def _(e):
                with e.Fori(0, NG // NB) as c:
                    for b in range(NB):
                        t = NB * c + b
                        e.wait_ge(fin, t + 1 + FIN_FREE - NB)
                        e.dma_start(xa[b][:], block_of(hist, t)).then_inc(ld[b], 16)
                        e.dma_start(xb[b][:], block_of(hist, t + T)).then_inc(ld[b], 16)

            @block.scalar
            def _(e):
                with e.Fori(0, NG // NB) as c:
                    for b in range(NB):
                        e.wait_ge(fin, NB * c + b + 1 + FIN_FREE)
                        e.dma_start(block_of(out_g, NB * c + b), res[b][:]).then_inc(written[b], 16)
                for b in range(NB):
                    e.wait_ge(written[b], 16 * (NG // NB))

            @block.vector
            def _(e):
                with e.Fori(0, NG // NB) as c:
                    for b in range(NB):
                        t = NB * c + b
                        e.wait_ge(ld[b], 32 * (c + 1))
                        e.tensor_tensor(xa[b][:], xa[b][:], xb[b][:], ALU.add).then_inc(sum_out, 1)
                        e.wait_ge(sum_out, t + 1)
                        for j in range(GROUP):
                            ins = e.bn_stats(st[b % 2][:, j, :], xa[b][:, j, :])
                        ins.then_inc(bn_out, 1)
                        e.wait_ge(fin, t + FIN_FREE - 1)
                        hold_dve(e, bn_out, t + 1)
                        for j in range(GROUP):
                            ins = e.bn_aggr(mv[b % 2][:, j, :], st[b % 2][:, j, :])
                        ins.then_inc(mv_out, 1)

            @block.gpsimd
            def _(e):
                e.sem_inc(fin, FIN_FREE)
                with e.Fori(0, NG // NB) as c:
                    for b in range(NB):
                        t = NB * c + b
                        e.wait_ge(written[b], 16 * c)
                        hold_pool(e, mv_out, t + 1)
                        layernorm_on_pool(e, chain, 4 * t, mv[b % 2], inv, xa[b], res[b], fin)
                        e.wait_ge(fin, FIN_FREE + t + 1)


FFB = [0, 1, 2, 0, 1, 2, 0, 1]
FIN_FREE = 4


def kernel(**inputs):
    import numpy as np
    import concourse.bacc as bacc
    from concourse.bass_utils import run_bass_kernel_spmd

    nc = bacc.Bacc("TRN2", target_bir_lowering=False, num_devices=1)
    names = ["x", "adj", "L0_gnn_Wq", "L0_gnn_Wk", "L0_gnn_Wv", "L0_gnn_Wo", "L1_gnn_attn_w", "L1_gnn_attn_b",
             "L1_gnn_W1", "L1_gnn_b1", "L1_gnn_W2", "L1_gnn_b2", "L1_gnn_g1", "L1_gnn_beta1", "L1_gnn_g2",
             "L1_gnn_beta2"]
    arrays, args = {}, []
    for name in names:
        a = np.ascontiguousarray(inputs[name])
        arrays[f"in_{name}"] = a
        args.append(nc.dram_tensor(f"in_{name}", a.shape, mybir.dt.from_np(a.dtype), kind="ExternalInput").ap())
    out = nc.dram_tensor("out", arrays["in_x"].shape, F32, kind="ExternalOutput").ap()
    gnn_kernel(nc, *args, out)
    result = run_bass_kernel_spmd(nc, [arrays], core_ids=[0])
    return result.results[0]["out"]
```

```python
from contextlib import ExitStack

import concourse.bass as bass
from concourse import mybir

F32 = mybir.dt.float32
F32R = mybir.dt.float32r
I32 = mybir.dt.int32
ALU = mybir.AluOpType
ACT = mybir.ActivationFunctionType
AX = mybir.AxisListType

P = 128
GROUP = 4
EPS = 1e-5
MASKED = -1e30
START = 1
LOWEST = -3.0e38


def split_product(pe, out, w, x, w_of, x_of):
    terms = [(a, b, k) for k in range(2) for a, b in ((0, 0), (0, 1), (1, 0))]
    for n, (a, b, k) in enumerate(terms):
        last = pe.matmul(out, w_of(w[a], k), x_of(x[b], k), start=(n == 0), stop=(n == len(terms) - 1))
    return last


def gnn_kernel(nc, x_in, adj, Wq, Wk, Wv, Wo, attn_w, attn_b, W1, b1, W2, b2, g1, beta1, g2, beta2, out):
    B, N, D = x_in.shape
    L, F = b1.shape
    NH = 8
    DK = D // NH
    KT = D // P
    FT = F // P
    NG = B // GROUP
    TOK = GROUP * N
    T = L * NG
    SCALE = 1.0 / float(DK) ** 0.5
    assert N == P and KT == 2 and TOK == 512 and FT == 8 and NG % 2 == 0

    hist = nc.dram_tensor("hist", [T + NG, GROUP, N, D], F32).ap()
    mask_hist = nc.dram_tensor("mask_hist", [NG, GROUP, N, N], F32).ap()
    x_g = x_in.rearrange("(t j) p d -> t j p d", j=GROUP)
    adj_g = adj.rearrange("(t j) p m -> t j p m", j=GROUP)
    out_g = out.rearrange("(t j) p d -> t j p d", j=GROUP)

    def layer_of(t):
        l = t >> (NG.bit_length() - 1)
        return l if isinstance(l, int) else nc.s_assert_within(
            l, 0, L - 1, skip_runtime_bounds_check_because="t is a step, below L * NG")

    def block_of(dram, t):
        return dram[bass.ds(t, 1)].rearrange("o j p d -> p (o j) d")

    with ExitStack() as whole:
        def tensor_maker(ctx, stage=""):
            return lambda name, shape, dt=F32: ctx.enter_context(nc.sbuf_tensor(stage + name, shape, dt))

        def sem_maker(ctx):
            return lambda *names: [ctx.enter_context(nc.semaphore(n)) for n in names]

        sb, sems = tensor_maker(whole), sem_maker(whole)
        ps = whole.enter_context(nc.psum_tensor("ps", [P, 8, 512], F32))
        ident = sb("ident", [P, P])
        b1_cols = sb("b1_cols", [P, L, FT])
        affine = sb("affine", [P, L, 5, D])
        b2_rows = sb("b2_rows", [P, L, D])
        half_neg = sb("half_neg", [P, GROUP])
        w1_raw = sb("w1_raw", [P, KT, F])
        w2_raw = sb("w2_raw", [P, FT, D])
        ident_set, const_ld, w_ld, aff_set = sems("ident_set", "const_ld", "w_ld", "aff_set")
        stored = sems("stored_even", "stored_odd")

        def load_layer_weights(e, layer):
            e.dma_start(w1_raw[:], W1[bass.ds(layer, 1)].rearrange("o (k p) f -> p (o k) f", p=P)).then_inc(w_ld, 16)
            e.dma_start(w2_raw[:], W2[bass.ds(layer, 1)].rearrange("o (m p) d -> p (o m) d", p=P)).then_inc(w_ld, 16)

        fence_dve = sb("fence_dve", [P, 64])
        holds = {"dve": 0, "pool": 0}
        fence_pool = sb("fence_pool", [P, 64])

        def hold_dve(e, sem, value):
            e.wait_ge(sem, value)
            n = holds["dve"] = holds["dve"] + 1
            e.memset(fence_dve[:, n:n + 1], 0.0)

        def hold_pool(e, sem, value):
            e.wait_ge(sem, value)
            n = holds["pool"] = holds["pool"] + 1
            e.tensor_tensor(fence_pool[:, n:n + 1], half_neg[:, 0:1], half_neg[:, 0:1], ALU.add)

        def layernorm_on_pool(e, chain, n0, stats, inv, y, dest, done=None):
            e.tensor_scalar(inv[:, 0, :], stats[:, :, 1], EPS, None, ALU.add).then_inc(chain, 1)
            e.tensor_scalar(inv[:, 1, :], stats[:, :, 0], -1.0, None, ALU.mult).then_inc(chain, 1)
            e.wait_ge(chain, n0 + 1)
            e.tensor_tensor(inv[:, 2, :], inv[:, 0, :], half_neg[:], ALU.pow).then_inc(chain, 1)
            e.wait_ge(chain, n0 + 3)
            e.tensor_tensor(inv[:, 3, :], inv[:, 1, :], inv[:, 2, :], ALU.mult).then_inc(chain, 1)
            hold_pool(e, chain, n0 + 4)
            for j in range(GROUP):
                last = e.tensor_scalar(dest[:, j, :], y[:, j, 0:D], inv[:, 2, j:j + 1], inv[:, 3, j:j + 1],
                                       ALU.mult, ALU.add)
            last.then_inc(chain if done is None else done, 1)

        with ExitStack() as ctx:
            sb = tensor_maker(ctx, "att_")
            w_raw = sb("w_raw", [P, 4, KT, D])
            w_hi = sb("w_hi", [P, 4, KT, D], F32R)
            w_lo = sb("w_lo", [P, 4, KT, D], F32R)
            xl = [sb(f"xl{i}", [P, GROUP, D]) for i in range(2)]
            adjl = [sb(f"adjl{i}", [P, GROUP, N], I32) for i in range(2)]
            mask = [sb(f"mask{i}", [P, GROUP, N]) for i in range(2)]
            adj_f = sb("adj_f", [P, GROUP, N])
            eye_sum = sb("eye_sum", [P, GROUP, N])
            mask1 = [sb(f"mask1_{i}", [P, GROUP, N]) for i in range(2)]
            xT = [sb("xT_hi", [P, KT, TOK], F32R), sb("xT_lo", [P, KT, TOK], F32R)]
            qk = [sb(f"qk{i}", [P, 4, TOK]) for i in range(2)]
            VW = DK + 2
            v = [sb(f"v{i}", [P, GROUP, NH, VW]) for i in range(2)]
            probs = sb("probs", [P, NH, N])
            probsT = sb("probsT", [P, NH, N])
            peak = sb("peak", [P, NH])
            neg_peak = sb("neg_peak", [P, NH])
            rden = sb("rden", [P, NH])
            att = sb("att", [P, D])
            attT = [sb("attT_hi", [P, KT, N], F32R), sb("attT_lo", [P, KT, N], F32R)]
            y = [sb(f"ya{i}", [P, GROUP, D]) for i in range(2)]
            stats = sb("a_stats", [P, GROUP, 6])
            mv = [sb(f"mv{i}", [P, GROUP, 2]) for i in range(2)]
            inv = sb("a_inv", [P, 4, GROUP])
            xo = [sb(f"xo{i}", [P, GROUP, D]) for i in range(2)]

            wa_ld, wa_split = sems("wa_ld", "wa_split")
            x_ld = sems("x_ld_even", "x_ld_odd")
            mask1_st = sems("mask1_st_even", "mask1_st_odd")
            (masks_made, v_set, xT_made, xT_hi_out, xT_lo_out, proj_made, proj_out, s_made, scored, peaked,
             exped, pT_made, pT_out_b, pT_out_a, pv_made, den_inv, att_out, attT_made, attT_hi_out,
             attT_lo_out, wo_made, y_out, bn_out, mv_out, ln_chain, ln_out, eye_made, eye_added) = sems(
                "masks_made", "v_set", "xT_made", "xT_hi_out", "xT_lo_out", "proj_made", "proj_out", "s_made",
                "scored", "peaked", "exped", "pT_made", "pT_out_b", "pT_out_a", "pv_made", "den_inv", "att_out",
                "attT_made", "attT_hi_out", "attT_lo_out", "wo_made", "y_out", "bn_out", "mv_out", "ln_chain",
                "ln_out", "eye_made", "eye_added")

            S = ps[:, 0:4, 0:2 * N]
            A = [ps[:, 4, :], ps[:, 5, :]]
            PB = [ps[:, 6, :], ps[:, 7, :]]

            def steps(e, body, tail=1):
                with e.Fori(0, NG // 2 - 1) as q:
                    for par in range(2):
                        body(q, par, True)
                body(NG // 2 - 1, 0, True)
                body(NG // 2 - 1, 1, False)

            block = ctx.enter_context(nc.Block())

            @block.sync
            def _(e):
                def load(t, par):
                    e.dma_start(xl[par][:], block_of(x_g, t)).then_inc(x_ld[par], 16)
                    e.dma_start(adjl[par][:], block_of(adj_g, t)).then_inc(x_ld[par], 16)

                for sem in stored + mask1_st:
                    e.sem_inc(sem, START)
                for n, w in enumerate((Wq, Wk, Wv, Wo)):
                    e.dma_start(w_raw[:, n], w.rearrange("(k p) n -> p k n", p=P)).then_inc(wa_ld, 16)
                load(0, 0)
                load(1, 1)
                load_layer_weights(e, 0)

                def body(q, par, more):
                    t = 2 * q + par
                    e.wait_ge(masks_made, 2 * (t + 1))
                    e.dma_start(block_of(mask_hist, t), mask1[par][:]).then_inc(mask1_st[par], 16)
                    if more:
                        e.wait_ge(y_out, START + GROUP * (t + 1))
                        load(t + 2, par)
                    e.wait_ge(ln_out, START + t + 1)
                    e.dma_start(block_of(hist, t), xo[par][:]).then_inc(stored[par], 16)

                with e.Fori(0, NG // 2 - 1) as q:
                    for par in range(2):
                        body(q, par, True)
                body(NG // 2 - 1, 0, False)
                body(NG // 2 - 1, 1, False)
                for par in range(2):
                    e.wait_ge(mask1_st[par], START + 16 * (NG // 2))
                    e.wait_ge(stored[par], START + 16 * (NG // 2))

            @block.gpsimd
            def _(e):
                e.memset(ident[:], 0.0).then_inc(eye_made, 1)
                e.wait_ge(eye_made, 1)
                e.affine_select(out=ident[:], in_=ident[:], compare_op=ALU.not_equal, fill=1.0, base=0,
                                pattern=[[-1, P]], channel_multiplier=1).then_inc(ident_set, 1)
                e.memset(half_neg[:], -0.5).then_inc(eye_made, 1)
                for par in range(2):
                    e.memset(v[par][:], 1.0).then_inc(v_set, 1)
                e.sem_inc(ln_out, START)
                e.wait_ge(eye_made, 2)
                e.wait_ge(ident_set, 1)

                def make_masks(q1, par, t1):
                    hold_pool(e, x_ld[par], 32 * (q1 + 1))
                    e.tensor_scalar(mask[par][:], adjl[par][:], 0.0, MASKED, ALU.is_equal, ALU.mult).then_inc(masks_made, 1)
                    e.tensor_scalar(adj_f[:], adjl[par][:], 1.0, None, ALU.mult).then_inc(eye_added, 1)
                    e.wait_ge(eye_added, 2 * t1 + 1)
                    for j in range(GROUP):
                        ins = e.tensor_tensor(eye_sum[:, j, :], adj_f[:, j, :], ident[:], ALU.add)
                    ins.then_inc(eye_added, 1)
                    hold_pool(e, eye_added, 2 * t1 + 2)
                    hold_pool(e, mask1_st[par], START + 16 * q1)
                    e.tensor_scalar(mask1[par][:], eye_sum[:], 0.0, MASKED, ALU.is_le, ALU.mult).then_inc(masks_made, 1)

                make_masks(0, 0, 0)
                e.wait_ge(const_ld, 16 * 6 * L)
                e.tensor_tensor(affine[:, :, 2, :], affine[:, :, 1, :], b2_rows[:], ALU.add).then_inc(aff_set, 1)

                def body(q, par, more):
                    t = 2 * q + par
                    if more:
                        e.wait_ge(masks_made, 2 * (t + 1))
                        e.wait_ge(peaked, GROUP * t + 1)
                        make_masks(q + (par + 1) // 2, 1 - par, t + 1)
                    e.wait_ge(stored[par], START + 16 * q)
                    hold_pool(e, mv_out, t + 1)
                    layernorm_on_pool(e, ln_chain, 4 * t, mv[par], inv, y[par], xo[par], ln_out)
                    e.wait_ge(ln_out, START + t + 1)

                steps(e, body)

            @block.tensor
            def _(e):
                e.wait_ge(ident_set, 1)
                e.wait_ge(wa_split, 2)

                def transpose_x(q1, par, k):
                    if k == 0:
                        e.wait_ge(x_ld[par], 32 * (q1 + 1))
                    for j in range(GROUP):
                        mm = e.transpose(A[k][:, j * N:(j + 1) * N], xl[par][:, j, k * P:(k + 1) * P], ident[:])
                    mm.then_inc(xT_made, 1)

                def project(t1, par, n):
                    bank = A[n % 2]
                    if n == 0:
                        e.wait_ge(xT_hi_out, 2 * (t1 + 1))
                        e.wait_ge(xT_lo_out, 2 * (t1 + 1))
                    if n >= 2:
                        e.wait_ge(proj_out, 6 * t1 + n - 1)
                    if n < 4:
                        mm = split_product(e, bank, (w_hi, w_lo), xT,
                                           lambda w, k: w[:, n % 2, k, (n // 2) * P:(n // 2 + 1) * P],
                                           lambda x, k: x[:, k, :])
                    else:
                        for h in range(2):
                            j = 2 * (n - 4) + h
                            mm = split_product(e, bank[:, h * D:(h + 1) * D], xT, (w_hi, w_lo),
                                               lambda x, k: x[:, k, j * N:(j + 1) * N],
                                               lambda w, k: w[:, 2, k, :])
                    mm.then_inc(proj_made, 1)

                def scores(par, j, last_k=None):
                    for h in range(NH):
                        r, c = h % 4, h // 4
                        if h == 4 and last_k is not None:
                            e.wait_ge(proj_out, last_k)
                        rows = slice(DK * r, DK * (r + 1))
                        mm = e.matmul(S[:, r, c * N:(c + 1) * N], qk[par][rows, 2 * c, j * N:(j + 1) * N],
                                      qk[par][rows, 2 * c + 1, j * N:(j + 1) * N], start=True, stop=True)
                    mm.then_inc(s_made, 1)

                def fill(q, par, j, half):
                    if j == 0:
                        transpose_x(q + (par + 1) // 2, 1 - par, half)
                    else:
                        project(2 * q + par + 1, 1 - par, 2 * (j - 1) + half)

                def body(q, par, more):
                    t = 2 * q + par
                    for j in range(GROUP):
                        i = GROUP * t + j
                        e.wait_ge(exped, 2 * i + 1)
                        for h in range(4, 8):
                            mm = e.transpose(PB[1][:, (h - 4) * N:(h - 3) * N], probs[:, h, :], ident[:])
                        mm.then_inc(pT_made, 1)
                        e.wait_ge(exped, 2 * i + 2)
                        e.wait_ge(y_out, START + i)
                        for h in range(4):
                            mm = e.transpose(PB[0][:, h * N:(h + 1) * N], probs[:, h, :], ident[:])
                        mm.then_inc(pT_made, 1)
                        if j < GROUP - 1:
                            scores(par, j + 1)
                        elif more:
                            scores(1 - par, 0, 6 * (t + 1) + 4)
                        e.wait_ge(pT_out_a, i + 1)
                        e.wait_ge(pT_out_b, i + 1)
                        if j == 0:
                            e.wait_ge(proj_out, 6 * (t + 1))
                        for h in range(NH):
                            mm = e.matmul(PB[0][:, h * VW:(h + 1) * VW], probsT[:, h, :], v[par][:, j, h, :],
                                          start=True, stop=True)
                        mm.then_inc(pv_made, 1)
                        if more:
                            fill(q, par, j, 0)
                        e.wait_ge(att_out, i + 1)
                        for k in range(KT):
                            mm = e.transpose(PB[1][:, k * N:(k + 1) * N], att[:, k * P:(k + 1) * P], ident[:])
                        mm.then_inc(attT_made, 1)
                        if more:
                            fill(q, par, j, 1)
                        e.wait_ge(attT_hi_out, i + 1)
                        e.wait_ge(attT_lo_out, i + 1)
                        split_product(e, PB[0][:, 0:D], attT, (w_hi, w_lo), lambda x, k: x[:, k, :],
                                      lambda w, k: w[:, 3, k, :]).then_inc(wo_made, 1)

                for k in range(KT):
                    transpose_x(0, 0, k)
                for n in range(4):
                    project(0, 0, n)
                e.wait_ge(proj_out, 4)
                scores(0, 0)
                project(0, 0, 4)
                project(0, 0, 5)
                steps(e, body)

            @block.scalar
            def _(e):
                with nc.allow_non_contiguous_dma(reason="columns of b1, once"):
                    for l in range(L):
                        e.dma_start(b1_cols[:, l, :], b1[l].rearrange("(m p) -> p m", p=P)).then_inc(const_ld, 16)
                for l in range(L):
                    for n, c in ((0, g1), (1, beta1), (3, g2), (4, beta2)):
                        e.dma_start(affine[:, l, n, :], c[l:l + 1, :].to_broadcast([P, D])).then_inc(const_ld, 16)
                    e.dma_start(b2_rows[:, l, :], b2[l:l + 1, :].to_broadcast([P, D])).then_inc(const_ld, 16)

                def xT_hi(t1, k):
                    e.wait_ge(xT_made, 2 * t1 + k + 1)
                    e.copy(xT[0][:, k, :], A[k]).then_inc(xT_hi_out, 1)

                def proj_copy(t1, par, n):
                    e.wait_ge(proj_made, 6 * t1 + n + 1)
                    if n < 4:
                        e.copy(qk[par][:, n, :], A[n % 2]).then_inc(proj_out, 1)
                    else:
                        for h in range(2):
                            ins = e.copy(v[par][:, 2 * (n - 4) + h, :, 0:DK],
                                         A[n % 2][:, h * D:(h + 1) * D].rearrange("p (h d) -> p h d", d=DK))
                        ins.then_inc(proj_out, 1)

                def copy_fill(t1, par1, j, half):
                    if j == 0:
                        xT_hi(t1, half)
                    else:
                        proj_copy(t1, par1, 2 * (j - 1) + half)

                def exps(i, half):
                    for h in range(4 - 4 * half, 8 - 4 * half):
                        ins = e.activation(probs[:, h, :], probs[:, h, :], ACT.Exp, bias=neg_peak[:, h:h + 1], scale=SCALE)
                    ins.then_inc(exped, 1)

                def body(q, par, more):
                    t = 2 * q + par
                    for j in range(GROUP):
                        i = GROUP * t + j
                        if j > 0 and more:
                            copy_fill(t + 1, 1 - par, j - 1, 0)
                            copy_fill(t + 1, 1 - par, j - 1, 1)
                        elif j == 0:
                            copy_fill(t, par, GROUP - 1, 0)
                            copy_fill(t, par, GROUP - 1, 1)
                        e.wait_ge(pT_made, 2 * i + 1)
                        e.copy(probsT[:, 4:8, :].rearrange("p h n -> p (h n)"), PB[1]).then_inc(pT_out_b, 1)
                        if more or j < GROUP - 1:
                            e.wait_ge(peaked, i + 2)
                            exps(i + 1, 0)
                        e.wait_ge(attT_made, i + 1)
                        e.copy(attT[0][:].rearrange("p k n -> p (k n)"), PB[1][:, 0:D]).then_inc(attT_hi_out, 1)
                        if more or j < GROUP - 1:
                            exps(i + 1, 1)

                for k in range(KT):
                    xT_hi(0, k)
                for n in range(4):
                    proj_copy(0, 0, n)
                e.wait_ge(v_set, 2)
                e.wait_ge(peaked, 1)
                exps(0, 0)
                exps(0, 1)
                steps(e, body)

            @block.vector
            def _(e):
                e.sem_inc(y_out, START)
                e.wait_ge(wa_ld, 64)
                e.tensor_copy(w_hi[:], w_raw[:]).then_inc(wa_split, 1)
                e.wait_ge(wa_split, 1)
                e.tensor_tensor(w_lo[:], w_raw[:], w_hi[:].bitcast(F32), ALU.subtract).then_inc(wa_split, 1)

                def xT_lo(t1):
                    for k in range(KT):
                        e.wait_ge(xT_hi_out, 2 * t1 + k + 1)
                        e.tensor_tensor(xT[1][:, k, :], A[k], xT[0][:, k, :].bitcast(F32), ALU.subtract).then_inc(xT_lo_out, 1)

                def masked_scores(i, t_, par, j):
                    e.wait_ge(s_made, i + 1)
                    hold_dve(e, masks_made, 2 * t_ + 1)
                    for h in range(NH):
                        r, c = h % 4, h // 4
                        ins = e.tensor_tensor_reduce(out=probs[:, h, :], in0=S[:, r, c * N:(c + 1) * N],
                                                     in1=mask[par][:, j, :], scale=1.0, scalar=LOWEST,
                                                     op0=ALU.add, op1=ALU.max, accum_out=peak[:, h:h + 1])
                    ins.then_inc(scored, 1)
                    e.wait_ge(scored, i + 1)
                    e.tensor_scalar(neg_peak[:], peak[:], -SCALE, None, ALU.mult).then_inc(peaked, 1)

                def body(q, par, more):
                    t = 2 * q + par
                    for j in range(GROUP):
                        i = GROUP * t + j
                        e.wait_ge(pT_made, 2 * i + 2)
                        e.tensor_copy(probsT[:, 0:4, :].rearrange("p h n -> p (h n)"), PB[0]).then_inc(pT_out_a, 1)
                        if more and j == 1:
                            xT_lo(t + 1)
                        if j < GROUP - 1:
                            masked_scores(i + 1, t, par, j + 1)
                        elif more:
                            masked_scores(i + 1, t + 1, 1 - par, 0)
                        e.wait_ge(pv_made, i + 1)
                        pv = PB[0][:, 0:NH * VW].rearrange("p (h w) -> p h w", w=VW)
                        e.reciprocal(rden[:], pv[:, :, DK]).then_inc(den_inv, 1)
                        e.wait_ge(den_inv, i + 1)
                        e.scalar_tensor_tensor(out=att[:].rearrange("p (h d) -> p h d", d=DK), in0=pv[:, :, 0:DK],
                                               scalar=0.0, in1=rden[:].rearrange("p (h o) -> p h o", o=1).to_broadcast([P, NH, DK]),
                                               op0=ALU.max, op1=ALU.mult).then_inc(att_out, 1)
                        e.wait_ge(attT_hi_out, i + 1)
                        e.tensor_tensor(attT[1][:].rearrange("p k n -> p (k n)"), PB[1][:, 0:D],
                                        attT[0][:].rearrange("p k n -> p (k n)").bitcast(F32),
                                        ALU.subtract).then_inc(attT_lo_out, 1)
                        if j == 0:
                            e.wait_ge(ln_out, START + 2 * q)
                        e.wait_ge(wo_made, i + 1)
                        e.tensor_tensor(y[par][:, j, :], PB[0][:, 0:D], xl[par][:, j, :], ALU.add).then_inc(y_out, 1)
                        e.wait_ge(y_out, START + i + 1)
                        e.bn_stats(stats[:, j, :], y[par][:, j, :]).then_inc(bn_out, 1)
                    hold_dve(e, bn_out, GROUP * (t + 1))
                    for j in range(GROUP):
                        ins = e.bn_aggr(mv[par][:, j, :], stats[:, j, :])
                    ins.then_inc(mv_out, 1)

                xT_lo(0)
                masked_scores(0, 0, 0, 0)
                steps(e, body)

        with ExitStack() as ctx:
            sb = tensor_maker(ctx, "gnn_")
            W = [sb("w1_hi", [P, KT, F], F32R), sb("w1_lo", [P, KT, F], F32R)]
            V = [sb("w2_hi", [P, FT, D], F32R), sb("w2_lo", [P, FT, D], F32R)]
            XW = D + 2
            x = [sb(f"x{i}", [P, GROUP, XW]) for i in range(2)]
            mask = [sb(f"gmask{i}", [P, GROUP, N]) for i in range(2)]
            aw = [sb(f"aw{i}", [P, 2, D]) for i in range(2)]
            ab = [sb(f"ab{i}", [P, 1]) for i in range(2)]
            warm = sb("warm", [P, 2])
            junk = sb("junk", [P, GROUP, 2, D])
            s_i = sb("s_i", [P, GROUP])
            s_j = sb("s_j", [P, GROUP])
            u = sb("u", [P, GROUP, N])
            top = sb("top", [P, GROUP])
            small = sb("small", [P, 5, GROUP])
            e1 = sb("e1", [P, GROUP, N])
            e2 = sb("e2", [P, GROUP, N])
            pT = sb("pT", [P, GROUP, N])
            rden = sb("grden", [P, GROUP])
            y1 = sb("res1", [P, GROUP, D])
            y2 = sb("res2", [P, GROUP, D])
            norm = sb("norm", [P, GROUP, D])
            h = sb("h", [P, GROUP, D])
            hb = [sb(f"hb{i}", [P, GROUP, D]) for i in range(2)]
            hT = [sb("hT_hi", [P, KT, TOK], F32R), sb("hT_lo", [P, KT, TOK], F32R)]
            g = [sb("g_hi", [P, FT, TOK], F32R), sb("g_lo", [P, FT, TOK], F32R)]
            st1 = sb("st1", [P, GROUP, 6])
            st2 = sb("st2", [P, GROUP, 6])
            mv1 = sb("mv1", [P, GROUP, 2])
            mv2 = sb("mv2", [P, GROUP, 2])
            inv = sb("ginv", [P, 4, GROUP])
            xo = [sb(f"gxo{i}", [P, GROUP, D]) for i in range(2)]

            g_ld = sems("g_ld_even", "g_ld_odd")
            (w_hi_set, w_split, x_ones, ff1_made, gelu_out, g_lo_out, pT_made, pT_out, agg_made, aij_out, sjT_made,
             u_out, bias_step, bias_out, exp_out, p_out, recip_out, y1_out, bn1_out, mv1_out, ln1, h_out, hb_out,
             hT_made, hT_hi_out, hT_lo_out, ff2_made, y2_out, bn2_out, mv2_out, ln2, norm2_out, x_out) = sems(
                *("g_" + n for n in (
                    "w_hi_set", "w_split", "x_ones", "ff1_made", "gelu_out", "g_lo_out", "pT_made", "pT_out",
                    "agg_made", "aij_out", "sjT_made", "u_out", "bias_step", "bias_out", "exp_out", "p_out",
                    "recip_out", "y1_out", "bn1_out", "mv1_out", "ln1", "h_out", "hb_out", "hT_made", "hT_hi_out",
                    "hT_lo_out", "ff2_made", "y2_out", "bn2_out", "mv2_out", "ln2", "norm2_out", "x_out")))

            FF1 = [ps[:, i, :] for i in range(3)]
            FF2 = [ps[:, 3, 0:D], ps[:, 4, 0:D]]
            AGG = [ps[:, 5, :], ps[:, 6, :]]
            TB = ps[:, 7, :]
            HT = [TB, AGG[0]]

            def steps(e, new_layer, body):
                pairs = NG // 2
                with e.Fori(0, L - 1) as l:
                    new_layer(l, True)
                    with e.Fori(0, pairs) as p:
                        for par in range(2):
                            body(l * pairs + p, par, True, True)
                new_layer(L - 1, False)
                with e.Fori((L - 1) * pairs, L * pairs - 1) as q:
                    for par in range(2):
                        body(q, par, True, True)
                body(L * pairs - 1, 0, True, False)
                body(L * pairs - 1, 1, False, False)

            def ahead(q, par, d):
                return 2 * q + (par + d), (par + d) % 2, q + (par + d) // 2

            block = ctx.enter_context(nc.Block())

            @block.sync
            def _(e):
                def load(t, par, half):
                    e.wait_ge(stored[par], START + 16 * (half + 1))
                    e.dma_start(x[par][:, :, 0:D], block_of(hist, t)).then_inc(g_ld[par], 16)
                    e.dma_start(mask[par][:], block_of(mask_hist, t & (NG - 1))).then_inc(g_ld[par], 16)
                    l = layer_of(t)
                    e.dma_start(aw[par][:].rearrange("p a d -> p (a d)"),
                                attn_w[bass.ds(l, 1), :].to_broadcast([P, 2 * D])).then_inc(g_ld[par], 16)
                    e.dma_start(ab[par][:], attn_b[bass.ds(l, 1)].rearrange("(a o) -> a o", o=1).to_broadcast([P, 1])).then_inc(g_ld[par], 16)

                def body(q, par, more=True):
                    t = 2 * q + par
                    if more:
                        t1, p1, h1 = ahead(q, par, 1)
                        t3, p3, h3 = ahead(q, par, 3)
                        e.wait_ge(y1_out, GROUP * (t1 + 1))
                        load(t3, p3, h3)
                    e.wait_ge(x_out, t + 1)
                    e.dma_start(block_of(hist, t + NG), xo[par][:]).then_inc(stored[par], 16)

                for t in range(2):
                    load(t, t, 0)
                e.wait_ge(y1_out, GROUP)
                load(2, 0, 1)
                pairs = NG // 2
                with e.Fori(0, L - 1) as l:
                    e.wait_ge(w_split, 2 * (l + 1))
                    load_layer_weights(e, l + 1)
                    with e.Fori(0, pairs) as p:
                        for par in range(2):
                            body(l * pairs + p, par)
                with e.Fori((L - 1) * pairs, L * pairs - 2) as q:
                    for par in range(2):
                        body(q, par)
                body(L * pairs - 2, 0)
                body(L * pairs - 2, 1, False)
                body(L * pairs - 1, 0, False)
                body(L * pairs - 1, 1, False)
                for par in range(2):
                    e.wait_ge(stored[par], START + 16 * (T + NG) // 2)

            @block.gpsimd
            def _(e):
                for par in range(2):
                    e.memset(x[par][:, :, D:XW], 1.0).then_inc(x_ones, 1)
                e.sem_inc(norm2_out, START)
                e.wait_ge(aff_set, 1)

                def row(l, n):
                    return affine[:, bass.ds(l, 1), n, :].to_broadcast([P, GROUP, D])

                def ln_attention(t1, par1):
                    l = layer_of(t1)
                    hold_pool(e, mv1_out, t1 + 1)
                    layernorm_on_pool(e, ln1, 6 * t1, mv1, inv, y1, norm)
                    e.wait_ge(ln1, 6 * t1 + 5)
                    e.tensor_tensor(norm[:], norm[:], row(l, 0), ALU.mult).then_inc(ln1, 1)
                    e.wait_ge(ln1, 6 * t1 + 6)
                    if not isinstance(t1, int):
                        e.wait_ge(hT_made, 2 * t1)
                    e.tensor_tensor(h[:], norm[:], row(l, 1), ALU.add).then_inc(h_out, 1)
                    e.tensor_tensor(hb[par1][:], norm[:], row(l, 2), ALU.add).then_inc(hb_out, 1)
                    e.wait_ge(hb_out, t1 + 1)

                def ln_ffn(t, par, half):
                    l = layer_of(t)
                    hold_pool(e, mv2_out, t + 1)
                    layernorm_on_pool(e, ln2, 5 * t, mv2, inv, y2, norm, norm2_out)
                    e.wait_ge(norm2_out, START + t + 1)
                    e.tensor_tensor(norm[:], norm[:], row(l, 3), ALU.mult).then_inc(ln2, 1)
                    e.wait_ge(ln2, 5 * t + 5)
                    e.wait_ge(stored[par], START + 16 * (half + NG // 2))
                    e.tensor_tensor(xo[par][:], norm[:], row(l, 4), ALU.add).then_inc(x_out, 1)
                    e.wait_ge(x_out, t + 1)

                def body(q, par, a1, a2):
                    if a1:
                        t1, p1, _ = ahead(q, par, 1)
                        ln_attention(t1, p1)
                    ln_ffn(2 * q + par, par, q)

                ln_attention(0, 0)
                steps(e, lambda l, more: None, body)

            @block.tensor
            def _(e):
                def probs_T(t1):
                    e.wait_ge(p_out, t1 + 1)
                    for j in range(GROUP):
                        mm = e.transpose(TB[:, j * N:(j + 1) * N], e1[:, j, :], ident[:])
                    mm.then_inc(pT_made, 1)

                def aggregate(t1, par1, j):
                    if j == 0:
                        e.wait_ge(pT_out, t1 + 1)
                    if j >= 2:
                        e.wait_ge(y1_out, GROUP * t1 + j - 1)
                    e.matmul(AGG[j % 2][:, 0:XW], pT[:, j, :], x[par1][:, j, :], start=True, stop=True).then_inc(agg_made, 1)

                def spread_sj(t2):
                    e.wait_ge(aij_out, t2 + 1)
                    for j in range(GROUP):
                        mm = e.transpose(TB[:, j * N:(j + 1) * N], s_j[:, j:j + 1].to_broadcast([P, N]), ident[:])
                    mm.then_inc(sjT_made, 1)

                def transpose_h(t1):
                    e.wait_ge(h_out, t1 + 1)
                    for k in range(KT):
                        for j in range(GROUP):
                            mm = e.transpose(HT[k][:, j * N:(j + 1) * N], h[:, j, k * P:(k + 1) * P], ident[:])
                        mm.then_inc(hT_made, 1)

                def ffn2(t, j):
                    e.wait_ge(y2_out, START + GROUP * t + (j - 1 if j >= 2 else 0))
                    terms = [(m, a, b) for m in range(FT) for a, b in ((0, 0), (0, 1), (1, 0))]
                    for n, (m, a, b) in enumerate(terms):
                        if j == 0 and (a, b) == (0, 0):
                            e.wait_ge(g_lo_out, FT * t + m + 1)
                        mm = e.matmul(FF2[j % 2], g[a][:, m, j * N:(j + 1) * N], V[b][:, m, :],
                                      start=(n == 0), stop=(n == len(terms) - 1))
                    mm.then_inc(ff2_made, 1)

                def body(q, par, a1, a2):
                    t = 2 * q + par
                    t1, p1, _ = ahead(q, par, 1)
                    e.wait_ge(hT_hi_out, 2 * (t + 1))
                    e.wait_ge(hT_lo_out, 2 * (t + 1))
                    if a1:
                        probs_T(t1)
                    e.wait_ge(w_split, 2 * (layer_of(t) + 1))
                    for m in range(FT):
                        if m >= 3:
                            e.wait_ge(g_lo_out, FT * t + m - 2)
                        split_product(e, FF1[FFB[m]], W, hT, lambda w, k: w[:, k, m * P:(m + 1) * P],
                                      lambda x_, k: x_[:, k, :]).then_inc(ff1_made, 1)
                        if a1:
                            for j in {0: (0, 1), 3: (2,), 4: (3,)}.get(m, ()):
                                aggregate(t1, p1, j)
                    for j in range(GROUP):
                        if j == 1 and a2:
                            spread_sj(t + 2)
                        if j == 3 and a1:
                            if a2:
                                e.wait_ge(u_out, t + 3)
                            transpose_h(t1)
                        ffn2(t, j)

                e.wait_ge(x_ones, 2)
                spread_sj(0)
                probs_T(0)
                for j in range(GROUP):
                    aggregate(0, 0, j)
                spread_sj(1)
                e.wait_ge(u_out, 2)
                transpose_h(0)

                steps(e, lambda l, more: None, body)

            @block.scalar
            def _(e):
                def copy_pT(t1):
                    e.wait_ge(pT_made, t1 + 1)
                    e.copy(pT[:].rearrange("p j n -> p (j n)"), TB).then_inc(pT_out, 1)

                def exps(t2):
                    e.wait_ge(bias_out, t2 + 1)
                    for j in range(GROUP):
                        e.activation(e1[:, j, :], u[:, j, :], ACT.Exp, bias=small[:, 3, j:j + 1])
                        ins = e.activation(e2[:, j, :], u[:, j, :], ACT.Exp, bias=small[:, 4, j:j + 1], scale=0.2)
                    ins.then_inc(exp_out, 1)

                def hT_hi(t1):
                    for k in range(KT):
                        e.wait_ge(hT_made, 2 * t1 + k + 1)
                        e.copy(hT[0][:, k, :], HT[k]).then_inc(hT_hi_out, 1)

                def body(q, par, a1, a2):
                    t = 2 * q + par
                    l = layer_of(t)
                    if a1:
                        copy_pT(t + 1)
                    for m in range(FT):
                        e.wait_ge(ff1_made, 8 * t + m + 1)
                        bias = b1_cols[:, bass.ds(l, 1), m]
                        e.activation(g[0][:, m, :], FF1[FFB[m]], ACT.Gelu, bias=bias)
                        e.activation(FF1[FFB[m]], FF1[FFB[m]], ACT.Gelu, bias=bias).then_inc(gelu_out, 1)
                    if a2:
                        exps(t + 2)
                        e.activation(warm[:, par:par + 1], half_neg[:, 0:1], ACT.Gelu)
                    if a1:
                        hT_hi(t + 1)

                exps(0)
                copy_pT(0)
                exps(1)
                hT_hi(0)
                steps(e, lambda l, more: None, body)

            @block.vector
            def _(e):
                def attention_sums(t2, par2, half2, j):
                    if j == 0:
                        e.wait_ge(g_ld[par2], 64 * (half2 + 1))
                    for n, s in ((0, s_i), (1, s_j)):
                        ins = e.tensor_tensor_reduce(out=junk[:, j, n, :], in0=x[par2][:, j, 0:D], in1=aw[par2][:, n, :],
                                                     scale=1.0, scalar=0.0, op0=ALU.mult, op1=ALU.add,
                                                     accum_out=s[:, j:j + 1])
                    if j == GROUP - 1:
                        ins.then_inc(aij_out, 1)

                def masked_sums(t2, par2):
                    hold_dve(e, sjT_made, t2 + 1)
                    for j in range(GROUP):
                        ins = e.tensor_tensor_reduce(out=u[:, j, :], in0=TB[:, j * N:(j + 1) * N], in1=mask[par2][:, j, :],
                                                     scale=1.0, scalar=LOWEST, op0=ALU.add, op1=ALU.max,
                                                     accum_out=top[:, j:j + 1])
                    ins.then_inc(u_out, 1)
                    e.wait_ge(aij_out, t2 + 1)
                    e.tensor_scalar(small[:, 0, :], s_i[:], ab[par2][:, 0:1], None, ALU.add).then_inc(bias_step, 1)
                    e.wait_ge(bias_step, 3 * t2 + 1)
                    e.wait_ge(u_out, t2 + 1)
                    e.tensor_tensor(small[:, 1, :], top[:], small[:, 0, :], ALU.add).then_inc(bias_step, 1)
                    e.wait_ge(bias_step, 3 * t2 + 2)
                    e.scalar_tensor_tensor(out=small[:, 2, :], in0=small[:, 1, :], scalar=0.2, in1=small[:, 1, :],
                                           op0=ALU.mult, op1=ALU.max).then_inc(bias_step, 1)
                    e.wait_ge(bias_step, 3 * t2 + 3)
                    e.tensor_tensor(small[:, 3, :], small[:, 0, :], small[:, 2, :], ALU.subtract)
                    e.scalar_tensor_tensor(out=small[:, 4, :], in0=small[:, 0, :], scalar=0.2, in1=small[:, 2, :],
                                           op0=ALU.mult, op1=ALU.subtract).then_inc(bias_out, 1)

                def probs_max(t1):
                    e.wait_ge(exp_out, t1 + 1)
                    e.tensor_tensor(e1[:], e1[:], e2[:], ALU.max).then_inc(p_out, 1)

                def residual1(t1, par1, j):
                    n = GROUP * t1 + j
                    bank = AGG[j % 2]
                    e.wait_ge(agg_made, n + 1)
                    e.reciprocal(rden[:, j:j + 1], bank[:, D:D + 1]).then_inc(recip_out, 1)
                    e.wait_ge(recip_out, n + 1)
                    e.scalar_tensor_tensor(out=y1[:, j, :], in0=bank[:, 0:D], scalar=rden[:, j:j + 1],
                                           in1=x[par1][:, j, 0:D], op0=ALU.mult, op1=ALU.add).then_inc(y1_out, 1)

                def stats1(t1, j):
                    e.wait_ge(y1_out, GROUP * t1 + j + 1)
                    e.bn_stats(st1[:, j, :], y1[:, j, :]).then_inc(bn1_out, 1)

                def mean_variance1(t1):
                    hold_dve(e, bn1_out, GROUP * (t1 + 1))
                    for j in range(GROUP):
                        ins = e.bn_aggr(mv1[:, j, :], st1[:, j, :])
                    ins.then_inc(mv1_out, 1)

                def residual2(t, par, j):
                    n = GROUP * t + j
                    if j == 0:
                        e.wait_ge(hb_out, t + 1)
                        e.wait_ge(norm2_out, START + t)
                    e.wait_ge(ff2_made, n + 1)
                    e.tensor_tensor(y2[:, j, :], FF2[j % 2], hb[par][:, j, :], ALU.add).then_inc(y2_out, 1)

                def stats2(t, j):
                    e.wait_ge(y2_out, START + GROUP * t + j + 1)
                    e.bn_stats(st2[:, j, :], y2[:, j, :]).then_inc(bn2_out, 1)

                def gelu_lo(t, m):
                    e.wait_ge(gelu_out, 8 * t + m + 1)
                    e.tensor_tensor(g[1][:, m, :], FF1[FFB[m]], g[0][:, m, :].bitcast(F32), ALU.subtract).then_inc(g_lo_out, 1)

                def hT_lo(t1):
                    for k in range(KT):
                        e.wait_ge(hT_hi_out, 2 * t1 + k + 1)
                        e.tensor_tensor(hT[1][:, k, :], HT[k], hT[0][:, k, :].bitcast(F32), ALU.subtract).then_inc(hT_lo_out, 1)

                def body(q, par, a1, a2):
                    t = 2 * q + par
                    t1, p1, _ = ahead(q, par, 1)
                    t2, p2, h2 = ahead(q, par, 2)
                    for m in range(FT):
                        gelu_lo(t, m)
                        if a1 and m == 0:
                            e.wait_ge(h_out, t1)
                        if a1 and m < GROUP:
                            residual1(t1, p1, m)
                        if a1 and 1 <= m <= GROUP:
                            stats1(t1, m - 1)
                        if a1 and m == GROUP:
                            mean_variance1(t1)
                        if a2 and m >= 6:
                            for j in range(2 * (m - 6), 2 * (m - 5)):
                                attention_sums(t2, p2, h2, j)
                    residual2(t, par, 0)
                    if a2:
                        masked_sums(t2, p2)
                    residual2(t, par, 1)
                    stats2(t, 0)
                    stats2(t, 1)
                    if a2:
                        probs_max(t2)
                    residual2(t, par, 2)
                    stats2(t, 2)
                    if a1:
                        hT_lo(t1)
                    residual2(t, par, 3)
                    stats2(t, 3)
                    hold_dve(e, bn2_out, GROUP * (t + 1))
                    for j in range(GROUP):
                        ins = e.bn_aggr(mv2[:, j, :], st2[:, j, :])
                    ins.then_inc(mv2_out, 1)

                def new_layer(l, more):
                    e.wait_ge(w_ld, 32 * (l + 1))
                    e.tensor_copy(W[0][:], w1_raw[:]).then_inc(w_hi_set, 1)
                    e.tensor_copy(V[0][:], w2_raw[:]).then_inc(w_hi_set, 1)
                    e.wait_ge(w_hi_set, 2 * l + 1)
                    e.tensor_tensor(W[1][:], w1_raw[:], W[0][:].bitcast(F32), ALU.subtract).then_inc(w_split, 1)
                    e.wait_ge(w_hi_set, 2 * l + 2)
                    e.tensor_tensor(V[1][:], w2_raw[:], V[0][:].bitcast(F32), ALU.subtract).then_inc(w_split, 1)

                e.sem_inc(y2_out, START)
                for j in range(GROUP):
                    attention_sums(0, 0, 0, j)
                masked_sums(0, 0)
                probs_max(0)
                for j in range(GROUP):
                    residual1(0, 0, j)
                    stats1(0, j)
                mean_variance1(0)
                for j in range(GROUP):
                    attention_sums(1, 1, 0, j)
                masked_sums(1, 1)
                probs_max(1)
                hT_lo(0)
                steps(e, new_layer, body)

        with ExitStack() as ctx:
            sb = tensor_maker(ctx, "fin_")
            NB = 4
            xa = [sb(f"xa{i}", [P, GROUP, D]) for i in range(NB)]
            xb = [sb(f"xb{i}", [P, GROUP, D]) for i in range(NB)]
            res = [sb(f"res{i}", [P, GROUP, D]) for i in range(NB)]
            st = [sb(f"fst{i}", [P, GROUP, 6]) for i in range(2)]
            mv = [sb(f"fmv{i}", [P, GROUP, 2]) for i in range(2)]
            inv = sb("finv", [P, 4, GROUP])
            ld = sems(*(f"f_ld{i}" for i in range(NB)))
            written = sems(*(f"f_written{i}" for i in range(NB)))
            sum_out, bn_out, mv_out, chain, fin = sems("f_sum", "f_bn", "f_mv", "f_chain", "f_fin")
            block = ctx.enter_context(nc.Block())

            @block.sync
            def _(e):
                with e.Fori(0, NG // NB) as c:
                    for b in range(NB):
                        t = NB * c + b
                        e.wait_ge(fin, t + 1 + FIN_FREE - NB)
                        e.dma_start(xa[b][:], block_of(hist, t)).then_inc(ld[b], 16)
                        e.dma_start(xb[b][:], block_of(hist, t + T)).then_inc(ld[b], 16)

            @block.scalar
            def _(e):
                for sem in written:
                    e.sem_inc(sem, START)
                with e.Fori(0, NG // NB) as c:
                    for b in range(NB):
                        e.wait_ge(fin, NB * c + b + 1 + FIN_FREE)
                        e.dma_start(block_of(out_g, NB * c + b), res[b][:]).then_inc(written[b], 16)
                for b in range(NB):
                    e.wait_ge(written[b], START + 16 * (NG // NB))

            @block.vector
            def _(e):
                with e.Fori(0, NG // NB) as c:
                    for b in range(NB):
                        t = NB * c + b
                        e.wait_ge(ld[b], 32 * (c + 1))
                        e.tensor_tensor(xa[b][:], xa[b][:], xb[b][:], ALU.add).then_inc(sum_out, 1)
                        e.wait_ge(sum_out, t + 1)
                        for j in range(GROUP):
                            ins = e.bn_stats(st[b % 2][:, j, :], xa[b][:, j, :])
                        ins.then_inc(bn_out, 1)
                        e.wait_ge(fin, t + FIN_FREE - 1)
                        hold_dve(e, bn_out, t + 1)
                        for j in range(GROUP):
                            ins = e.bn_aggr(mv[b % 2][:, j, :], st[b % 2][:, j, :])
                        ins.then_inc(mv_out, 1)

            @block.gpsimd
            def _(e):
                e.sem_inc(fin, FIN_FREE)
                with e.Fori(0, NG // NB) as c:
                    for b in range(NB):
                        t = NB * c + b
                        e.wait_ge(written[b], START + 16 * c)
                        hold_pool(e, mv_out, t + 1)
                        layernorm_on_pool(e, chain, 4 * t, mv[b % 2], inv, xa[b], res[b], fin)
                        e.wait_ge(fin, FIN_FREE + t + 1)


FFB = [0, 1, 2, 0, 1, 2, 0, 1]
FIN_FREE = 4


def kernel(**inputs):
    import numpy as np
    import concourse.bacc as bacc
    from concourse.bass_utils import run_bass_kernel_spmd

    nc = bacc.Bacc("TRN2", target_bir_lowering=False, num_devices=1)
    names = ["x", "adj", "L0_gnn_Wq", "L0_gnn_Wk", "L0_gnn_Wv", "L0_gnn_Wo", "L1_gnn_attn_w", "L1_gnn_attn_b",
             "L1_gnn_W1", "L1_gnn_b1", "L1_gnn_W2", "L1_gnn_b2", "L1_gnn_g1", "L1_gnn_beta1", "L1_gnn_g2",
             "L1_gnn_beta2"]
    arrays, args = {}, []
    for name in names:
        a = np.ascontiguousarray(inputs[name])
        arrays[f"in_{name}"] = a
        args.append(nc.dram_tensor(f"in_{name}", a.shape, mybir.dt.from_np(a.dtype), kind="ExternalInput").ap())
    out = nc.dram_tensor("out", arrays["in_x"].shape, F32, kind="ExternalOutput").ap()
    gnn_kernel(nc, *args, out)
    result = run_bass_kernel_spmd(nc, [arrays], core_ids=[0])
    return result.results[0]["out"]
```

```python
from contextlib import ExitStack

import concourse.bass as bass
from concourse import mybir

F32 = mybir.dt.float32
F32R = mybir.dt.float32r
I32 = mybir.dt.int32
ALU = mybir.AluOpType
ACT = mybir.ActivationFunctionType

P = 128
GROUP = 4
EPS = 1e-5
MASKED = -1e30
FFB = [0, 1, 2, 0, 1, 2, 0, 1]
START = 1
LOWEST = -3.0e38


def split_product(pe, out, w, x, w_of, x_of, ks=(0, 1)):
    terms = [(a, b, k) for k in ks for a, b in ((0, 0), (0, 1), (1, 0))]
    for n, (a, b, k) in enumerate(terms):
        last = pe.matmul(out, w_of(w[a], k), x_of(x[b], k), start=(n == 0 and k == 0),
                         stop=(n == len(terms) - 1 and k == 1))
    return last


def gnn_kernel(nc, x_in, adj, Wq, Wk, Wv, Wo, attn_w, attn_b, W1, b1, W2, b2, g1, beta1, g2, beta2, out):
    B, N, D = x_in.shape
    L, F = b1.shape
    NH = 8
    DK = D // NH
    KT = D // P
    FT = F // P
    NG = B // GROUP
    TOK = GROUP * N
    T = L * NG
    SCALE = 1.0 / float(DK) ** 0.5
    assert N == P and KT == 2 and TOK == 512 and FT == 8 and NG % 2 == 0

    hist = nc.dram_tensor("hist", [T + NG, GROUP, N, D], F32).ap()
    mask_hist = nc.dram_tensor("mask_hist", [NG, GROUP, N, N], F32).ap()
    x_g = x_in.rearrange("(t j) p d -> t j p d", j=GROUP)
    adj_g = adj.rearrange("(t j) p m -> t j p m", j=GROUP)
    out_g = out.rearrange("(t j) p d -> t j p d", j=GROUP)

    def layer_of(t):
        l = t >> (NG.bit_length() - 1)
        return l if isinstance(l, int) else nc.s_assert_within(
            l, 0, L - 1, skip_runtime_bounds_check_because="t is a step, below L * NG")

    def block_of(dram, t):
        return dram[bass.ds(t, 1)].rearrange("o j p d -> p (o j) d")

    with ExitStack() as whole:
        def tensor_maker(ctx, stage=""):
            return lambda name, shape, dt=F32: ctx.enter_context(nc.sbuf_tensor(stage + name, shape, dt))

        def sem_maker(ctx):
            return lambda *names: [ctx.enter_context(nc.semaphore(n)) for n in names]

        sb, sems = tensor_maker(whole), sem_maker(whole)
        ps = whole.enter_context(nc.psum_tensor("ps", [P, 8, 512], F32))
        ident = sb("ident", [P, P])
        b1_cols = sb("b1_cols", [P, L, FT])
        affine = sb("affine", [P, L, 5, D])
        b2_rows = sb("b2_rows", [P, L, D])
        half_neg = sb("half_neg", [P, GROUP])
        w1_raw = sb("w1_raw", [P, KT, F])
        w2_raw = sb("w2_raw", [P, FT, D])
        y = [sb(f"y{i}", [P, GROUP, D]) for i in range(2)]
        mv = [sb(f"mv{i}", [P, GROUP, 2]) for i in range(2)]
        inv = sb("inv", [P, 4, GROUP])
        xo = [sb(f"xo{i}", [P, GROUP, D]) for i in range(2)]
        XW = D + 2
        gx = [sb(f"x{i}", [P, GROUP, XW]) for i in range(2)]
        gmask = [sb(f"gmask{i}", [P, GROUP, N]) for i in range(2)]
        aw = [sb(f"aw{i}", [P, 2, D]) for i in range(2)]
        ab = [sb(f"ab{i}", [P, 1]) for i in range(2)]
        g_ld = sems("g_ld_even", "g_ld_odd")
        mask1_st = sems("mask1_st_even", "mask1_st_odd")
        mv_out, ln_chain, ln_out = sems("mv_out", "ln_chain", "ln_out")
        ident_set, const_ld, w_ld, aff_set = sems("ident_set", "const_ld", "w_ld", "aff_set")
        stored = sems("stored_even", "stored_odd")

        def load_layer_weights(e, layer):
            e.dma_start(w1_raw[:], W1[bass.ds(layer, 1)].rearrange("o (k p) f -> p (o k) f", p=P)).then_inc(w_ld, 16)
            e.dma_start(w2_raw[:], W2[bass.ds(layer, 1)].rearrange("o (m p) d -> p (o m) d", p=P)).then_inc(w_ld, 16)

        def load_step(e, t, par, half):
            e.wait_ge(stored[par], START + 16 * (half + 1))
            e.dma_start(gx[par][:, :, 0:D], block_of(hist, t)).then_inc(g_ld[par], 16)
            e.dma_start(gmask[par][:], block_of(mask_hist, t & (NG - 1))).then_inc(g_ld[par], 16)
            l = layer_of(t)
            e.dma_start(aw[par][:].rearrange("p a d -> p (a d)"),
                        attn_w[bass.ds(l, 1), :].to_broadcast([P, 2 * D])).then_inc(g_ld[par], 16)
            e.dma_start(ab[par][:], attn_b[bass.ds(l, 1)].rearrange("(a o) -> a o", o=1).to_broadcast([P, 1])).then_inc(g_ld[par], 16)

        fence_dve = sb("fence_dve", [P, 192])
        holds = {"dve": 0, "pool": 0}
        fence_pool = sb("fence_pool", [P, 192])

        def hold_dve(e, sem, value):
            e.wait_ge(sem, value)
            n = holds["dve"] = holds["dve"] + 1
            e.memset(fence_dve[:, n:n + 1], 0.0)

        def hold_pool(e, sem, value):
            e.wait_ge(sem, value)
            n = holds["pool"] = holds["pool"] + 1
            e.tensor_tensor(fence_pool[:, n:n + 1], half_neg[:, 0:1], half_neg[:, 0:1], ALU.add)

        def layernorm_on_pool(e, chain, n0, stats, inv, y, dest, done=None):
            e.tensor_scalar(inv[:, 0, :], stats[:, :, 1], EPS, None, ALU.add).then_inc(chain, 1)
            e.tensor_scalar(inv[:, 1, :], stats[:, :, 0], -1.0, None, ALU.mult).then_inc(chain, 1)
            e.wait_ge(chain, n0 + 1)
            e.tensor_tensor(inv[:, 2, :], inv[:, 0, :], half_neg[:], ALU.pow).then_inc(chain, 1)
            e.wait_ge(chain, n0 + 3)
            e.tensor_tensor(inv[:, 3, :], inv[:, 1, :], inv[:, 2, :], ALU.mult).then_inc(chain, 1)
            hold_pool(e, chain, n0 + 4)
            for j in range(GROUP):
                last = e.tensor_scalar(dest[:, j, :], y[:, j, 0:D], inv[:, 2, j:j + 1], inv[:, 3, j:j + 1],
                                       ALU.mult, ALU.add)
            last.then_inc(chain if done is None else done, 1)

        def ln_group(e, t, par):
            hold_pool(e, mv_out, t + 1)
            layernorm_on_pool(e, ln_chain, 4 * t, mv[par], inv, y[par], xo[par], ln_out)
            e.wait_ge(ln_out, START + t + 1)

        with ExitStack() as ctx:
            sb = tensor_maker(ctx, "att_")
            w_raw = sb("w_raw", [P, 4, KT, D])
            w_hi = sb("w_hi", [P, 4, KT, D], F32R)
            w_lo = sb("w_lo", [P, 4, KT, D], F32R)
            xq = sb("xq", [P, GROUP, D])
            xl = [sb(f"xl{i}", [P, GROUP, D]) for i in range(2)]
            adjl = [sb(f"adjl{i}", [P, GROUP, N], I32) for i in range(2)]
            mask = [sb(f"mask{i}", [P, GROUP, N]) for i in range(2)]
            adj_f = sb("adj_f", [P, GROUP, N])
            eye_sum = sb("eye_sum", [P, GROUP, N])
            mask1 = [sb(f"mask1_{i}", [P, GROUP, N]) for i in range(2)]
            xT = [sb("xT_hi", [P, KT, TOK], F32R), sb("xT_lo", [P, KT, TOK], F32R)]
            qk = [sb(f"qk{i}", [P, 4, TOK]) for i in range(2)]
            v = [sb(f"v{i}", [P, GROUP, D]) for i in range(2)]
            probs = [sb(f"probs{i}", [P, NH, N]) for i in range(2)]
            probsT = sb("probsT", [P, NH, N])
            peak = [sb(f"peak{i}", [P, NH]) for i in range(2)]
            neg_peak = [sb(f"neg_peak{i}", [P, NH]) for i in range(2)]
            den = [sb(f"den{i}", [P, NH]) for i in range(2)]
            rden = sb("rden", [P, NH])
            rden_cols = sb("rden_cols", [P, NH, DK])
            rdenT = sb("rdenT", [P, KT, N])
            att = sb("att", [P, KT, N])
            attT = [sb("attT_hi", [P, KT, N], F32R), sb("attT_lo", [P, KT, N], F32R)]
            stats = sb("a_stats", [P, GROUP, 6])

            wa_ld = sems("wqk_ld", "wvo_ld")
            wa_split, xq_ld = sems("wa_split", "xq_ld")
            x_ld = sems("x_ld_even", "x_ld_odd")
            (masks_made, xT_made, xT_hi_out, xT_lo_out, proj_made, proj_out, s_made, scored, peaked, exped,
             pT_made, pT_out_b, pT_out_a, pv_made, den_inv, rden_out, rdenT_made, rdenT_out, att_out,
             attT_hi_out, attT_lo_out, wo_made, y_out, bn_out, eye_made, eye_added) = sems(
                "masks_made", "xT_made", "xT_hi_out", "xT_lo_out", "proj_made", "proj_out", "s_made", "scored",
                "peaked", "exped", "pT_made", "pT_out_b", "pT_out_a", "pv_made", "den_inv", "rden_out",
                "rdenT_made", "rdenT_out", "att_out", "attT_hi_out", "attT_lo_out", "wo_made", "y_out", "bn_out",
                "eye_made", "eye_added")

            S = ps[:, 0:4, 0:2 * N]
            A = [ps[:, 4, :], ps[:, 5, :]]
            PB = [ps[:, 6, :], ps[:, 7, :]]

            def steps(e, body, first=0):
                with e.Fori(first, NG // 2 - 1) as q:
                    for par in range(2):
                        body(q, par, True, True)
                body(NG // 2 - 1, 0, True, False)
                body(NG // 2 - 1, 1, False, False)

            def graphs(q, par, a1):
                t = 2 * q + par
                for j in range(GROUP):
                    if j + 2 < GROUP:
                        yield j, GROUP * t + j, True, (True, t, par, j + 2)
                    else:
                        yield j, GROUP * t + j, a1 or j + 1 < GROUP, (a1, t + 1, 1 - par, j + 2 - GROUP)

            block = ctx.enter_context(nc.Block())

            @block.sync
            def _(e):
                def load(t, par):
                    e.dma_start(xl[par][:], block_of(x_g, t)).then_inc(x_ld[par], 16)
                    e.dma_start(adjl[par][:], block_of(adj_g, t)).then_inc(x_ld[par], 16)

                for sem in stored + mask1_st:
                    e.sem_inc(sem, START)
                e.dma_start(xq[:], block_of(x_g, 0)).then_inc(xq_ld, 16)
                for n, w in ((0, Wq), (1, Wk)):
                    e.dma_start(w_raw[:, n], w.rearrange("(k p) n -> p k n", p=P)).then_inc(wa_ld[0], 16)
                load(0, 0)
                load(1, 1)
                e.wait_ge(xT_made, 2)
                e.dma_start(xq[:], block_of(x_g, 1)).then_inc(xq_ld, 16)
                load_layer_weights(e, 0)

                def body(q, par, more):
                    t = 2 * q + par
                    if more:
                        e.wait_ge(xT_made, 2 * (t + 2))
                        e.dma_start(xq[:], block_of(x_g, t + 2)).then_inc(xq_ld, 16)
                    e.wait_ge(masks_made, 2 * (t + 1))
                    e.dma_start(block_of(mask_hist, t), mask1[par][:]).then_inc(mask1_st[par], 16)
                    if more:
                        e.wait_ge(y_out, START + GROUP * (t + 1))
                        load(t + 2, par)
                    if not isinstance(t, int) or t < NG - 1:
                        e.wait_ge(ln_out, START + t + 1)
                        e.dma_start(block_of(hist, t), xo[par][:]).then_inc(stored[par], 16)

                with e.Fori(0, NG // 2 - 1) as q:
                    for par in range(2):
                        body(q, par, True)
                for t in range(2):
                    e.wait_ge(mask1_st[t], START + 16)
                    load_step(e, t, t, 0)
                body(NG // 2 - 1, 0, False)
                body(NG // 2 - 1, 1, False)
                for par in range(2):
                    e.wait_ge(mask1_st[par], START + 16 * (NG // 2))

            @block.gpsimd
            def _(e):
                e.memset(ident[:], 0.0).then_inc(eye_made, 1)
                e.wait_ge(eye_made, 1)
                e.affine_select(out=ident[:], in_=ident[:], compare_op=ALU.not_equal, fill=1.0, base=0,
                                pattern=[[-1, P]], channel_multiplier=1).then_inc(ident_set, 1)
                e.memset(half_neg[:], -0.5).then_inc(eye_made, 1)
                e.sem_inc(ln_out, START)
                e.wait_ge(eye_made, 2)
                e.wait_ge(ident_set, 1)

                def make_masks(q1, par, t1):
                    hold_pool(e, x_ld[par], 32 * (q1 + 1))
                    e.tensor_scalar(mask[par][:], adjl[par][:], 0.0, MASKED, ALU.is_equal, ALU.mult).then_inc(masks_made, 1)
                    e.tensor_scalar(adj_f[:], adjl[par][:], 1.0, None, ALU.mult).then_inc(eye_added, 1)
                    e.wait_ge(eye_added, 2 * t1 + 1)
                    for j in range(GROUP):
                        ins = e.tensor_tensor(eye_sum[:, j, :], adj_f[:, j, :], ident[:], ALU.add)
                    ins.then_inc(eye_added, 1)
                    hold_pool(e, eye_added, 2 * t1 + 2)
                    hold_pool(e, mask1_st[par], START + 16 * q1)
                    e.tensor_scalar(mask1[par][:], eye_sum[:], 0.0, MASKED, ALU.is_le, ALU.mult).then_inc(masks_made, 1)

                make_masks(0, 0, 0)
                e.wait_ge(const_ld, 16 * (5 + L))
                e.tensor_tensor(affine[:, :, 2, :], affine[:, :, 1, :], b2_rows[:], ALU.add).then_inc(aff_set, 1)

                def body(q, par, a1, a2):
                    t = 2 * q + par
                    if a1:
                        e.wait_ge(masks_made, 2 * (t + 1))
                        e.wait_ge(peaked, GROUP * t + 1)
                        make_masks(q + (par + 1) // 2, 1 - par, t + 1)
                    if isinstance(t, int) and t == NG - 1:
                        return
                    e.wait_ge(stored[par], START + 16 * q)
                    ln_group(e, t, par)

                steps(e, body)

            @block.tensor
            def _(e):
                e.wait_ge(ident_set, 1)

                def transpose_x(t1, k):
                    if k == 0:
                        e.wait_ge(xq_ld, 16 * (t1 + 1))
                    if not isinstance(t1, int) or t1:
                        e.wait_ge(proj_out, 6 * t1 - 1 + k)
                    for j in range(GROUP):
                        mm = e.transpose(A[k][:, j * N:(j + 1) * N], xq[:, j, k * P:(k + 1) * P], ident[:])
                    mm.then_inc(xT_made, 1)

                def project(t1, par, n, parts=(0, 1)):
                    bank = A[n % 2]
                    if n == 0 and 0 in parts:
                        e.wait_ge(xT_hi_out, 2 * (t1 + 1))
                        e.wait_ge(xT_lo_out, 2 * (t1 + 1))
                    if n >= 2 and 0 in parts:
                        e.wait_ge(proj_out, 6 * t1 + n - 1)
                    if n < 4:
                        mm = split_product(e, bank, (w_hi, w_lo), xT,
                                           lambda w, k: w[:, n % 2, k, (n // 2) * P:(n // 2 + 1) * P],
                                           lambda x, k: x[:, k, :], parts)
                    else:
                        for h in parts:
                            j = 2 * (n - 4) + h
                            mm = split_product(e, bank[:, h * D:(h + 1) * D], xT, (w_hi, w_lo),
                                               lambda x, k: x[:, k, j * N:(j + 1) * N],
                                               lambda w, k: w[:, 2, k, :])
                    if 1 in parts:
                        mm.then_inc(proj_made, 1)

                def scores(i, par, j):
                    for h in range(NH):
                        r, c = h % 4, h // 4
                        rows = slice(DK * r, DK * (r + 1))
                        mm = e.matmul(S[:, r, c * N:(c + 1) * N], qk[par][rows, 2 * c, j * N:(j + 1) * N],
                                      qk[par][rows, 2 * c + 1, j * N:(j + 1) * N], start=True, stop=True)
                    mm.then_inc(s_made, 1)

                def fill(t, par, j, half, a1, a2, parts=(0, 1)):
                    if j < 3 and a1:
                        project(t + 1, 1 - par, 2 * j + half, parts)
                    if j == 3 and half == 0 and a2:
                        for k in parts:
                            transpose_x(t + 2, k)

                def body(q, par, a1, a2):
                    t = 2 * q + par
                    for j, i, _, (has2, t2, par2, j2) in graphs(q, par, a1):
                        e.wait_ge(exped, 2 * i + 1)
                        e.wait_ge(rdenT_out, START + i)
                        for h in range(4, 8):
                            mm = e.transpose(PB[1][:, (h - 4) * N:(h - 3) * N], probs[j % 2][:, h, :], ident[:])
                        mm.then_inc(pT_made, 1)
                        fill(t, par, j, 0, a1, a2, parts=(0,))
                        e.wait_ge(exped, 2 * i + 2)
                        e.wait_ge(y_out, START + i)
                        for h in range(4):
                            mm = e.transpose(PB[0][:, h * N:(h + 1) * N], probs[j % 2][:, h, :], ident[:])
                        mm.then_inc(pT_made, 1)
                        fill(t, par, j, 0, a1, a2, parts=(1,))
                        e.wait_ge(pT_out_b, i + 1)
                        e.wait_ge(rden_out, i + 1)
                        for k in range(KT):
                            mm = e.transpose(PB[1][:, k * N:(k + 1) * N],
                                             rden_cols[:, 4 * k:4 * k + 4].rearrange("p h d -> p (h d)"), ident[:])
                        mm.then_inc(rdenT_made, 1)
                        e.wait_ge(pT_out_a, i + 1)
                        for h in range(NH):
                            rows = slice(DK * (h % 4), DK * (h % 4 + 1))
                            mm = e.matmul(PB[0][rows, h // 4 * N:(h // 4 + 1) * N], v[par][:, j, h * DK:(h + 1) * DK],
                                          probsT[:, h, :], start=True, stop=True)
                        mm.then_inc(pv_made, 1)
                        if has2:
                            e.wait_ge(scored, i + 2)
                            if j2 == 0:
                                e.wait_ge(proj_out, 6 * t2 + 4)
                            scores(i + 2, par2, j2)
                        fill(t, par, j, 1, a1, a2)
                        e.wait_ge(attT_hi_out, i + 1)
                        e.wait_ge(attT_lo_out, i + 1)
                        split_product(e, PB[0][:, 0:D], attT, (w_hi, w_lo), lambda x, k: x[:, k, :],
                                      lambda w, k: w[:, 3, k, :]).then_inc(wo_made, 1)

                for k in range(KT):
                    transpose_x(0, k)
                for n in range(6):
                    e.wait_ge(wa_split, 2 if n < 4 else 4)
                    project(0, 0, n)
                scores(0, 0, 0)
                for k in range(KT):
                    transpose_x(1, k)
                e.wait_ge(scored, 1)
                scores(1, 0, 1)
                steps(e, body)

            @block.scalar
            def _(e):
                e.sem_inc(rdenT_out, START)
                for n, w in ((2, Wv), (3, Wo)):
                    e.dma_start(w_raw[:, n], w.rearrange("(k p) n -> p k n", p=P)).then_inc(wa_ld[1], 16)

                def on_all(c):
                    return c.rearrange("(o l) d -> o l d", o=1).to_broadcast([P, L, D])

                def xT_hi(t1, k):
                    e.wait_ge(xT_made, 2 * t1 + k + 1)
                    e.copy(xT[0][:, k, :], A[k]).then_inc(xT_hi_out, 1)

                def proj_copy(t1, par, n):
                    e.wait_ge(proj_made, 6 * t1 + n + 1)
                    dest = qk[par][:, n, :] if n < 4 else v[par][:, 2 * (n - 4):2 * (n - 3), :].rearrange("p j d -> p (j d)")
                    e.copy(dest, A[n % 2]).then_inc(proj_out, 1)

                def exps(i, b, half):
                    for h in range(4 - 4 * half, 8 - 4 * half):
                        ins = e.activation(probs[b][:, h, :], probs[b][:, h, :], ACT.Exp, bias=neg_peak[b][:, h:h + 1],
                                           scale=SCALE, accum_out=den[b][:, h:h + 1])
                    ins.then_inc(exped, 1)

                def body(q, par, a1, a2):
                    t = 2 * q + par
                    for j, i, has1, _ in graphs(q, par, a1):
                        if j > 0 and a1:
                            proj_copy(t + 1, 1 - par, 2 * (j - 1))
                            proj_copy(t + 1, 1 - par, 2 * (j - 1) + 1)
                        e.wait_ge(pT_made, 2 * i + 1)
                        e.copy(probsT[:, 4:8, :].rearrange("p h n -> p (h n)"), PB[1]).then_inc(pT_out_b, 1)
                        if j == 3 and a2:
                            for k in range(KT):
                                xT_hi(t + 2, k)
                        if has1 and j < 3:
                            e.wait_ge(peaked, i + 2)
                            exps(i + 1, (j + 1) % 2, 0)
                        e.wait_ge(rdenT_made, i + 1)
                        e.copy(rdenT[:], PB[1][:, 0:D].rearrange("p (k n) -> p k n", k=KT)).then_inc(rdenT_out, 1)
                        if has1:
                            if j == 3:
                                e.wait_ge(peaked, i + 2)
                                exps(i + 1, (j + 1) % 2, 0)
                            exps(i + 1, (j + 1) % 2, 1)

                for k in range(KT):
                    xT_hi(0, k)
                for n, c in ((0, g1), (1, beta1), (3, g2), (4, beta2)):
                    e.dma_start(affine[:, :, n, :], on_all(c)).then_inc(const_ld, 16)
                e.dma_start(b2_rows[:], on_all(b2)).then_inc(const_ld, 16)
                with nc.allow_non_contiguous_dma(reason="columns of b1, once"):
                    for l in range(L):
                        e.dma_start(b1_cols[:, l, :], b1[l].rearrange("(m p) -> p m", p=P)).then_inc(const_ld, 16)
                for n in range(6):
                    proj_copy(0, 0, n)
                for k in range(KT):
                    xT_hi(1, k)
                e.wait_ge(peaked, 1)
                exps(0, 0, 0)
                exps(0, 0, 1)
                steps(e, body)

            @block.vector
            def _(e):
                e.sem_inc(y_out, START)

                def split_weights(n):
                    pair = slice(2 * n, 2 * n + 2)
                    e.wait_ge(wa_ld[n], 32)
                    e.tensor_copy(w_hi[:, pair], w_raw[:, pair]).then_inc(wa_split, 1)
                    e.wait_ge(wa_split, 2 * n + 1)
                    e.tensor_tensor(w_lo[:, pair], w_raw[:, pair], w_hi[:, pair].bitcast(F32), ALU.subtract).then_inc(wa_split, 1)

                def xT_lo(t1):
                    for k in range(KT):
                        e.wait_ge(xT_hi_out, 2 * t1 + k + 1)
                        e.tensor_tensor(xT[1][:, k, :], A[k], xT[0][:, k, :].bitcast(F32), ALU.subtract).then_inc(xT_lo_out, 1)

                def masked_scores(i, t_, par, j, between=None, at=NH):
                    if j == 0:
                        e.wait_ge(masks_made, 2 * t_ + 1)
                    hold_dve(e, s_made, i + 1)
                    for h in range(NH):
                        if h == at:
                            between()
                        r, c = h % 4, h // 4
                        ins = e.tensor_tensor_reduce(out=probs[j % 2][:, h, :], in0=S[:, r, c * N:(c + 1) * N],
                                                     in1=mask[par][:, j, :], scale=1.0, scalar=LOWEST,
                                                     op0=ALU.add, op1=ALU.max, accum_out=peak[j % 2][:, h:h + 1])
                    ins.then_inc(scored, 1)
                    if between and at == NH:
                        between()
                    e.wait_ge(scored, i + 1)
                    e.tensor_scalar(neg_peak[j % 2][:], peak[j % 2][:], -SCALE, None, ALU.mult).then_inc(peaked, 1)

                def statistics(i, par, j):
                    e.wait_ge(y_out, START + i + 1)
                    e.bn_stats(stats[:, j, :], y[par][:, j, :]).then_inc(bn_out, 1)
                    if j == GROUP - 1:
                        hold_dve(e, bn_out, i + 1)
                        for n in range(GROUP):
                            ins = e.bn_aggr(mv[par][:, n, :], stats[:, n, :])
                        ins.then_inc(mv_out, 1)

                def body(q, par, a1, a2, before=True):
                    t = 2 * q + par
                    for j, i, _, (has2, t2, par2, j2) in graphs(q, par, a1):
                        e.wait_ge(exped, 2 * i + 2)
                        e.reciprocal(rden[:], den[j % 2][:]).then_inc(den_inv, 1)
                        e.wait_ge(den_inv, i + 1)
                        e.tensor_copy(rden_cols[:], rden[:].rearrange("p (h o) -> p h o", o=1)
                                      .to_broadcast([P, NH, DK])).then_inc(rden_out, 1)
                        e.wait_ge(pT_made, 2 * i + 2)
                        e.tensor_copy(probsT[:, 0:4, :].rearrange("p h n -> p (h n)"), PB[0]).then_inc(pT_out_a, 1)
                        if j == 0 and before:
                            statistics(i - 1, 1 - par, GROUP - 1)
                        if j == 3 and a2:
                            xT_lo(t + 2)
                        e.wait_ge(rdenT_out, START + i + 1)
                        e.wait_ge(pv_made, i + 1)
                        e.scalar_tensor_tensor(out=att[:].rearrange("p k n -> p (k n)"), in0=PB[0][:, 0:D], scalar=0.0,
                                               in1=rdenT[:].rearrange("p k n -> p (k n)"), op0=ALU.max, op1=ALU.mult).then_inc(att_out, 1)
                        e.wait_ge(att_out, i + 1)
                        e.tensor_copy(attT[0][:], att[:]).then_inc(attT_hi_out, 1)
                        e.wait_ge(attT_hi_out, i + 1)
                        e.tensor_tensor(attT[1][:], att[:], attT[0][:].bitcast(F32), ALU.subtract).then_inc(attT_lo_out, 1)
                        if j == 0 and before:
                            e.wait_ge(ln_out, START + t - 1)
                        if j == 0:
                            e.wait_ge(x_ld[par], 32 * (q + 1))

                        def residual(i=i, j=j):
                            e.wait_ge(wo_made, i + 1)
                            e.tensor_tensor(y[par][:, j, :], PB[0][:, 0:D], xl[par][:, j, :], ALU.add).then_inc(y_out, 1)

                        if has2:
                            masked_scores(i + 2, t2, par2, j2, residual, at=4 if j == GROUP - 1 else NH)
                        else:
                            residual()
                        if j < GROUP - 1:
                            statistics(i, par, j)

                split_weights(0)
                xT_lo(0)
                split_weights(1)
                masked_scores(0, 0, 0, 0)
                xT_lo(1)
                masked_scores(1, 0, 0, 1)
                body(0, 0, True, True, before=False)
                body(0, 1, True, True)
                steps(e, body, first=1)
                statistics(B - 1, 1, GROUP - 1)

        with ExitStack() as ctx:
            sb = tensor_maker(ctx, "gnn_")
            W = [sb("w1_hi", [P, KT, F], F32R), sb("w1_lo", [P, KT, F], F32R)]
            V = [sb("w2_hi", [P, FT, D], F32R), sb("w2_lo", [P, FT, D], F32R)]
            x, mask = gx, gmask
            warm = sb("warm", [P, 2])
            junk = sb("junk", [P, GROUP, 2, D])
            s_i = sb("s_i", [P, GROUP])
            s_j = sb("s_j", [P, GROUP])
            u = sb("u", [P, GROUP, N])
            top = sb("top", [P, GROUP])
            small = sb("small", [P, 5, GROUP])
            e1 = sb("e1", [P, GROUP, N])
            e2 = sb("e2", [P, GROUP, N])
            pT = sb("pT", [P, GROUP, N])
            rden = sb("grden", [P, GROUP])
            y1 = sb("res1", [P, GROUP, D])
            y2 = sb("res2", [P, GROUP, D])
            norm = sb("norm", [P, GROUP, D])
            h = sb("h", [P, GROUP, D])
            hb = [sb(f"hb{i}", [P, GROUP, D]) for i in range(2)]
            hT = [sb("hT_hi", [P, KT, TOK], F32R), sb("hT_lo", [P, KT, TOK], F32R)]
            g = [sb("g_hi", [P, FT, TOK], F32R), sb("g_lo", [P, FT, TOK], F32R)]
            st1 = sb("st1", [P, GROUP, 6])
            st2 = sb("st2", [P, GROUP, 6])
            mv1 = sb("mv1", [P, GROUP, 2])
            mv2 = sb("mv2", [P, GROUP, 2])
            fin = [sb(f"fin{i}", [P, GROUP, D]) for i in range(2)]
            st3 = sb("st3", [P, GROUP, 6])
            mv3 = sb("mv3", [P, GROUP, 2])

            fin_ld = sems("fin_ld_even", "fin_ld_odd")
            out_stored = sems("out_stored_even", "out_stored_odd")
            fin_sum, bn3_out, mv3_out, ln3, fin_out = sems("fin_sum", "bn3_out", "mv3_out", "ln3", "fin_out")
            (w_hi_set, w_split, x_ones, ff1_made, gelu_out, g_lo_out, pT_made, pT_out, agg_made, aij_out, sjT_made,
             u_out, bias_step, bias_out, exp_out, p_out, recip_out, y1_out, bn1_out, mv1_out, ln1, h_out, hb_out,
             hT_made, hT_hi_out, hT_lo_out, ff2_made, y2_out, bn2_out, mv2_out, ln2, norm2_out, x_out) = sems(
                *("g_" + n for n in (
                    "w_hi_set", "w_split", "x_ones", "ff1_made", "gelu_out", "g_lo_out", "pT_made", "pT_out",
                    "agg_made", "aij_out", "sjT_made", "u_out", "bias_step", "bias_out", "exp_out", "p_out",
                    "recip_out", "y1_out", "bn1_out", "mv1_out", "ln1", "h_out", "hb_out", "hT_made", "hT_hi_out",
                    "hT_lo_out", "ff2_made", "y2_out", "bn2_out", "mv2_out", "ln2", "norm2_out", "x_out")))

            FF1 = [ps[:, i, :] for i in range(3)]
            FF2 = [ps[:, 3, 0:D], ps[:, 4, 0:D]]
            AGG = [ps[:, 5, :], ps[:, 6, :]]
            TB = ps[:, 7, :]
            HT = [TB, AGG[0]]

            FIRST = (L - 1) * NG

            def steps(e, body, new_layer=lambda l: None, peel_layer_end=False, peel_last_layer=False):
                pairs = NG // 2
                with e.Fori(0, L - 1) as l:
                    new_layer(l)
                    with e.Fori(0, pairs - peel_layer_end) as p:
                        for par in range(2):
                            body(l * pairs + p, par, True, True, False, False)
                    if peel_layer_end:
                        for par in range(2):
                            body(l * pairs + (pairs - 1), par, True, True, par == 1, False)
                new_layer(L - 1)
                first = (L - 1) * pairs
                if peel_last_layer:
                    for par in range(2):
                        body(first, par, True, True, False, par == 1)
                with e.Fori(first + peel_last_layer, L * pairs - 1) as q:
                    for par in range(2):
                        body(q, par, True, True, False, peel_last_layer)
                body(L * pairs - 1, 0, True, False, False, True)
                body(L * pairs - 1, 1, False, False, False, True)

            def ahead(q, par, d):
                return 2 * q + (par + d), (par + d) % 2, q + (par + d) // 2

            block = ctx.enter_context(nc.Block())

            @block.sync
            def _(e):
                def load_fin(t, par):
                    e.dma_start(fin[par][:], block_of(hist, t - FIRST)).then_inc(fin_ld[par], 16)

                def load_ahead(q, par):
                    _, _, h1 = ahead(q, par, 1)
                    t3, p3, h3 = ahead(q, par, 3)
                    e.wait_ge(y1_out, GROUP * (2 * q + par + 2))
                    load_step(e, t3, p3, h3)

                def store_x(q, par):
                    t = 2 * q + par
                    e.wait_ge(x_out, t + 1)
                    e.dma_start(block_of(hist, t + NG), xo[par][:]).then_inc(stored[par], 16)

                def store_out(q, par):
                    t1, p1, h1 = ahead(q, par, -1)
                    e.wait_ge(fin_out, START + t1 - FIRST + 1)
                    e.dma_start(block_of(out_g, t1 - FIRST), fin[p1][:]).then_inc(out_stored[p1], 16)
                    if not isinstance(q, int) or 2 * q + par + 1 < T:
                        e.wait_ge(out_stored[p1], 16 * (h1 - FIRST // 2 + 1))
                        load_fin(t1 + 2, p1)

                e.wait_ge(ln_out, START + NG)
                e.dma_start(block_of(hist, NG - 1), xo[1][:]).then_inc(stored[1], 16)
                for t in range(2):
                    e.dma_start(fin[t][:], block_of(hist, t)).then_inc(fin_ld[t], 16)
                e.wait_ge(y1_out, GROUP)
                load_step(e, 2, 0, 1)
                pairs = NG // 2
                with e.Fori(0, L - 1) as l:
                    e.wait_ge(w_split, 2 * (l + 1))
                    load_layer_weights(e, l + 1)
                    with e.Fori(0, pairs) as p:
                        for par in range(2):
                            load_ahead(l * pairs + p, par)
                            store_x(l * pairs + p, par)
                first = (L - 1) * pairs
                load_ahead(first, 0)
                load_ahead(first, 1)
                store_out(first, 1)
                with e.Fori(first + 1, L * pairs - 2) as q:
                    for par in range(2):
                        load_ahead(q, par)
                        store_out(q, par)
                load_ahead(L * pairs - 2, 0)
                for t in range(T - 4, T + 1):
                    store_out(t // 2, t % 2)
                for par in range(2):
                    e.wait_ge(stored[par], START + 16 * T // 2)
                    e.wait_ge(out_stored[par], 16 * NG // 2)

            @block.gpsimd
            def _(e):
                for par in range(2):
                    e.memset(x[par][:, :, D:XW], 1.0).then_inc(x_ones, 1)
                e.wait_ge(stored[1], START + 16 * (NG // 2 - 1))
                ln_group(e, NG - 1, 1)
                e.sem_inc(norm2_out, START)
                e.sem_inc(fin_out, START)
                e.wait_ge(aff_set, 1)

                def row(l, n):
                    return affine[:, bass.ds(l, 1), n, :].to_broadcast([P, GROUP, D])

                def ln_attention(t1, par1):
                    l = layer_of(t1)
                    hold_pool(e, mv1_out, t1 + 1)
                    layernorm_on_pool(e, ln1, 6 * t1, mv1, inv, y1, norm)
                    e.wait_ge(ln1, 6 * t1 + 5)
                    e.tensor_tensor(norm[:], norm[:], row(l, 0), ALU.mult).then_inc(ln1, 1)
                    e.wait_ge(ln1, 6 * t1 + 6)
                    if not isinstance(t1, int):
                        e.wait_ge(hT_made, 2 * t1)
                    e.tensor_tensor(h[:], norm[:], row(l, 1), ALU.add).then_inc(h_out, 1)
                    e.tensor_tensor(hb[par1][:], norm[:], row(l, 2), ALU.add).then_inc(hb_out, 1)
                    e.wait_ge(hb_out, t1 + 1)

                def ln_ffn(t, par, half, last_layer):
                    l = layer_of(t)
                    hold_pool(e, mv2_out, t + 1)
                    layernorm_on_pool(e, ln2, 5 * t, mv2, inv, y2, norm, norm2_out)
                    e.wait_ge(norm2_out, START + t + 1)
                    e.tensor_tensor(norm[:], norm[:], row(l, 3), ALU.mult).then_inc(ln2, 1)
                    e.wait_ge(ln2, 5 * t + 5)
                    e.wait_ge(stored[par], START + 16 * (T // 2 if last_layer else half + NG // 2))
                    e.tensor_tensor(xo[par][:], norm[:], row(l, 4), ALU.add).then_inc(x_out, 1)
                    e.wait_ge(x_out, t + 1)

                def final_norm(t1, par1):
                    hold_pool(e, mv3_out, t1 - FIRST + 1)
                    layernorm_on_pool(e, ln3, 4 * (t1 - FIRST), mv3, inv, fin[par1], fin[par1], fin_out)
                    e.wait_ge(fin_out, START + t1 - FIRST + 1)

                def body(q, par, a1, a2, layer_end, final):
                    if a1:
                        t1, p1, _ = ahead(q, par, 1)
                        ln_attention(t1, p1)
                    if final:
                        t1, p1, _ = ahead(q, par, -1)
                        final_norm(t1, p1)
                    ln_ffn(2 * q + par, par, q, final or isinstance(q, int))

                ln_attention(0, 0)
                steps(e, body, peel_last_layer=True)
                final_norm(T - 1, 1)

            @block.tensor
            def _(e):
                def probs_T(t1):
                    e.wait_ge(p_out, t1 + 1)
                    for j in range(GROUP):
                        mm = e.transpose(TB[:, j * N:(j + 1) * N], e1[:, j, :], ident[:])
                    mm.then_inc(pT_made, 1)

                def aggregate(t1, par1, j):
                    if j == 0:
                        e.wait_ge(pT_out, t1 + 1)
                    if j >= 2:
                        e.wait_ge(y1_out, GROUP * t1 + j - 1)
                    e.matmul(AGG[j % 2][:, 0:XW], pT[:, j, :], x[par1][:, j, :], start=True, stop=True).then_inc(agg_made, 1)

                def spread_sj(t2):
                    e.wait_ge(aij_out, t2 + 1)
                    for j in range(GROUP):
                        mm = e.transpose(TB[:, j * N:(j + 1) * N], s_j[:, j:j + 1].to_broadcast([P, N]), ident[:])
                    mm.then_inc(sjT_made, 1)

                def transpose_h(t1):
                    e.wait_ge(h_out, t1 + 1)
                    for k in range(KT):
                        for j in range(GROUP):
                            mm = e.transpose(HT[k][:, j * N:(j + 1) * N], h[:, j, k * P:(k + 1) * P], ident[:])
                        mm.then_inc(hT_made, 1)

                def ffn2(t, j, a2):
                    e.wait_ge(y2_out, START + GROUP * t + (j - 1 if j >= 2 else 0))
                    terms = [(m, a, b) for m in range(FT) for a, b in ((0, 0), (0, 1), (1, 0))]
                    for n, (m, a, b) in enumerate(terms):
                        if j == 1 and m == FT // 2 and (a, b) == (0, 0) and a2:
                            spread_sj(t + 2)
                        if j == 0 and (a, b) == (0, 0):
                            e.wait_ge(g_lo_out, FT * t + m + 1)
                        mm = e.matmul(FF2[j % 2], g[a][:, m, j * N:(j + 1) * N], V[b][:, m, :],
                                      start=(n == 0), stop=(n == len(terms) - 1))
                    mm.then_inc(ff2_made, 1)

                def body(q, par, a1, a2, layer_end, final):
                    t = 2 * q + par
                    t1, p1, _ = ahead(q, par, 1)
                    e.wait_ge(hT_hi_out, 2 * (t + 1))
                    e.wait_ge(hT_lo_out, 2 * (t + 1))
                    if a1:
                        probs_T(t1)
                    e.wait_ge(w_split, 2 * layer_of(t) + 1)
                    for m in range(FT):
                        if m >= 3:
                            e.wait_ge(g_lo_out, FT * t + m - 2)
                        split_product(e, FF1[FFB[m]], W, hT, lambda w, k: w[:, k, m * P:(m + 1) * P],
                                      lambda x_, k: x_[:, k, :]).then_inc(ff1_made, 1)
                        if a1:
                            for j in {0: (0, 1), 3: (2,), 4: (3,)}.get(m, ()):
                                aggregate(t1, p1, j)
                    e.wait_ge(w_split, 2 * layer_of(t) + 2)
                    for j in range(GROUP):
                        if j == 3 and a1:
                            if a2:
                                e.wait_ge(u_out, t + 3)
                            transpose_h(t1)
                        ffn2(t, j, a2)

                e.wait_ge(x_ones, 2)
                spread_sj(0)
                probs_T(0)
                for j in range(GROUP):
                    aggregate(0, 0, j)
                spread_sj(1)
                e.wait_ge(u_out, 2)
                transpose_h(0)

                steps(e, body)

            @block.scalar
            def _(e):
                def copy_pT(t1):
                    e.wait_ge(pT_made, t1 + 1)
                    e.copy(pT[:].rearrange("p j n -> p (j n)"), TB).then_inc(pT_out, 1)

                def exps(t2):
                    e.wait_ge(bias_out, t2 + 1)
                    for j in range(GROUP):
                        e.activation(e1[:, j, :], u[:, j, :], ACT.Exp, bias=small[:, 3, j:j + 1])
                        ins = e.activation(e2[:, j, :], u[:, j, :], ACT.Exp, bias=small[:, 4, j:j + 1], scale=0.2)
                    ins.then_inc(exp_out, 1)

                def gelu_table(n):
                    e.activation(warm[:, n:n + 1], half_neg[:, 0:1], ACT.Gelu)

                def hT_hi(t1):
                    for k in range(KT):
                        e.wait_ge(hT_made, 2 * t1 + k + 1)
                        e.copy(hT[0][:, k, :], HT[k]).then_inc(hT_hi_out, 1)

                def body(q, par, a1, a2, layer_end, final):
                    t = 2 * q + par
                    l = layer_of(t)
                    if par == 0:
                        gelu_table(0)
                    if a1:
                        copy_pT(t + 1)
                    for m in range(FT):
                        e.wait_ge(ff1_made, 8 * t + m + 1)
                        bias = b1_cols[:, bass.ds(l, 1), m]
                        e.activation(g[0][:, m, :], FF1[FFB[m]], ACT.Gelu, bias=bias)
                        e.activation(FF1[FFB[m]], FF1[FFB[m]], ACT.Gelu, bias=bias).then_inc(gelu_out, 1)
                    if a2:
                        exps(t + 2)
                    if a1:
                        hT_hi(t + 1)
                        if par == 0:
                            gelu_table(1)

                exps(0)
                copy_pT(0)
                exps(1)
                hT_hi(0)
                steps(e, body)

            @block.vector
            def _(e):
                def attention_sums(t2, par2, half2, j):
                    if j == 0:
                        e.wait_ge(g_ld[par2], 64 * (half2 + 1))
                    for n, s in ((0, s_i), (1, s_j)):
                        ins = e.tensor_tensor_reduce(out=junk[:, j, n, :], in0=x[par2][:, j, 0:D], in1=aw[par2][:, n, :],
                                                     scale=1.0, scalar=0.0, op0=ALU.mult, op1=ALU.add,
                                                     accum_out=s[:, j:j + 1])
                    if j == GROUP - 1:
                        ins.then_inc(aij_out, 1)

                def masked_sums(t2, par2):
                    hold_dve(e, sjT_made, t2 + 1)
                    for j in range(GROUP):
                        ins = e.tensor_tensor_reduce(out=u[:, j, :], in0=TB[:, j * N:(j + 1) * N], in1=mask[par2][:, j, :],
                                                     scale=1.0, scalar=LOWEST, op0=ALU.add, op1=ALU.max,
                                                     accum_out=top[:, j:j + 1])
                    ins.then_inc(u_out, 1)
                    e.wait_ge(aij_out, t2 + 1)
                    e.tensor_scalar(small[:, 0, :], s_i[:], ab[par2][:, 0:1], None, ALU.add).then_inc(bias_step, 1)
                    e.wait_ge(bias_step, 3 * t2 + 1)
                    e.wait_ge(u_out, t2 + 1)
                    e.tensor_tensor(small[:, 1, :], top[:], small[:, 0, :], ALU.add).then_inc(bias_step, 1)
                    e.wait_ge(bias_step, 3 * t2 + 2)
                    e.scalar_tensor_tensor(out=small[:, 2, :], in0=small[:, 1, :], scalar=0.2, in1=small[:, 1, :],
                                           op0=ALU.mult, op1=ALU.max).then_inc(bias_step, 1)
                    e.wait_ge(bias_step, 3 * t2 + 3)
                    e.tensor_tensor(small[:, 3, :], small[:, 0, :], small[:, 2, :], ALU.subtract)
                    e.scalar_tensor_tensor(out=small[:, 4, :], in0=small[:, 0, :], scalar=0.2, in1=small[:, 2, :],
                                           op0=ALU.mult, op1=ALU.subtract).then_inc(bias_out, 1)

                def probs_max(t1):
                    e.wait_ge(exp_out, t1 + 1)
                    e.tensor_tensor(e1[:], e1[:], e2[:], ALU.max).then_inc(p_out, 1)

                def residual1(t1, par1, j):
                    n = GROUP * t1 + j
                    bank = AGG[j % 2]
                    e.wait_ge(agg_made, n + 1)
                    e.reciprocal(rden[:, j:j + 1], bank[:, D:D + 1]).then_inc(recip_out, 1)
                    e.wait_ge(recip_out, n + 1)
                    e.scalar_tensor_tensor(out=y1[:, j, :], in0=bank[:, 0:D], scalar=rden[:, j:j + 1],
                                           in1=x[par1][:, j, 0:D], op0=ALU.mult, op1=ALU.add).then_inc(y1_out, 1)

                def stats1(t1, j):
                    e.wait_ge(y1_out, GROUP * t1 + j + 1)
                    e.bn_stats(st1[:, j, :], y1[:, j, :]).then_inc(bn1_out, 1)

                def mean_variance1(t1):
                    hold_dve(e, bn1_out, GROUP * (t1 + 1))
                    for j in range(GROUP):
                        ins = e.bn_aggr(mv1[:, j, :], st1[:, j, :])
                    ins.then_inc(mv1_out, 1)

                def residual2(t, par, j):
                    n = GROUP * t + j
                    if j == 0:
                        e.wait_ge(hb_out, t + 1)
                        e.wait_ge(norm2_out, START + t)
                    e.wait_ge(ff2_made, n + 1)
                    e.tensor_tensor(y2[:, j, :], FF2[j % 2], hb[par][:, j, :], ALU.add).then_inc(y2_out, 1)

                def stats2(t, j):
                    e.wait_ge(y2_out, START + GROUP * t + j + 1)
                    e.bn_stats(st2[:, j, :], y2[:, j, :]).then_inc(bn2_out, 1)

                def gelu_lo(t, m):
                    e.wait_ge(gelu_out, 8 * t + m + 1)
                    e.tensor_tensor(g[1][:, m, :], FF1[FFB[m]], g[0][:, m, :].bitcast(F32), ALU.subtract).then_inc(g_lo_out, 1)

                def hT_lo(t1):
                    for k in range(KT):
                        e.wait_ge(hT_hi_out, 2 * t1 + k + 1)
                        e.tensor_tensor(hT[1][:, k, :], HT[k], hT[0][:, k, :].bitcast(F32), ALU.subtract).then_inc(hT_lo_out, 1)

                def final_sum(q, par):
                    t1, p1, h1 = ahead(q, par, -1)
                    e.wait_ge(x_out, t1 + 1)
                    e.wait_ge(fin_ld[p1], 16 * (h1 - FIRST // 2 + 1))
                    e.tensor_tensor(fin[p1][:], fin[p1][:], xo[p1][:], ALU.add).then_inc(fin_sum, 1)

                def final_statistics(q, par):
                    t1, p1, _ = ahead(q, par, -1)
                    n = t1 - FIRST
                    e.wait_ge(fin_sum, n + 1)
                    for j in range(GROUP):
                        ins = e.bn_stats(st3[:, j, :], fin[p1][:, j, :])
                    ins.then_inc(bn3_out, 1)
                    e.wait_ge(fin_out, START + n)
                    hold_dve(e, bn3_out, n + 1)
                    for j in range(GROUP):
                        ins = e.bn_aggr(mv3[:, j, :], st3[:, j, :])
                    ins.then_inc(mv3_out, 1)

                def split_w1(l, n):
                    k = n % 2
                    if n < 2:
                        if n == 0:
                            e.wait_ge(w_ld, 32 * (l + 1))
                        e.tensor_copy(W[0][:, k, :], w1_raw[:, k, :]).then_inc(w_hi_set, 1)
                    else:
                        e.wait_ge(w_hi_set, 3 * l + k + 1)
                        ins = e.tensor_tensor(W[1][:, k, :], w1_raw[:, k, :], W[0][:, k, :].bitcast(F32), ALU.subtract)
                        if n == 3:
                            ins.then_inc(w_split, 1)

                def body(q, par, a1, a2, layer_end, final):
                    t = 2 * q + par
                    t1, p1, _ = ahead(q, par, 1)
                    t2, p2, h2 = ahead(q, par, 2)
                    for m in range(FT):
                        gelu_lo(t, m)
                        if a1 and m == 0:
                            e.wait_ge(h_out, t1)
                        if a1 and m < GROUP:
                            residual1(t1, p1, m)
                        if a1 and 1 <= m <= GROUP:
                            stats1(t1, m - 1)
                        if a1 and m == GROUP:
                            mean_variance1(t1)
                        if a2:
                            for j in {5: (0,), 6: (1,), 7: (2, 3)}.get(m, ()):
                                attention_sums(t2, p2, h2, j)
                    residual2(t, par, 0)
                    if a2:
                        masked_sums(t2, p2)
                    if final:
                        final_sum(q, par)
                    if layer_end:
                        split_w1(layer_of(t1), 0)
                    residual2(t, par, 1)
                    if layer_end:
                        split_w1(layer_of(t1), 1)
                    if final:
                        final_statistics(q, par)
                    if a2:
                        probs_max(t2)
                    residual2(t, par, 2)
                    if layer_end:
                        split_w1(layer_of(t1), 2)
                        split_w1(layer_of(t1), 3)
                    if a1:
                        hT_lo(t1)
                    for j in range(3):
                        stats2(t, j)
                    residual2(t, par, 3)
                    stats2(t, 3)
                    hold_dve(e, bn2_out, GROUP * (t + 1))
                    for j in range(GROUP):
                        ins = e.bn_aggr(mv2[:, j, :], st2[:, j, :])
                    ins.then_inc(mv2_out, 1)

                def new_layer(l):
                    e.wait_ge(w_ld, 32 * (l + 1))
                    e.tensor_copy(V[0][:], w2_raw[:]).then_inc(w_hi_set, 1)
                    e.wait_ge(w_hi_set, 3 * l + 3)
                    e.tensor_tensor(V[1][:], w2_raw[:], V[0][:].bitcast(F32), ALU.subtract).then_inc(w_split, 1)

                e.sem_inc(y2_out, START)
                for j in range(GROUP):
                    attention_sums(0, 0, 0, j)
                masked_sums(0, 0)
                split_w1(0, 0)
                split_w1(0, 1)
                probs_max(0)
                split_w1(0, 2)
                split_w1(0, 3)
                for j in range(GROUP):
                    residual1(0, 0, j)
                    stats1(0, j)
                mean_variance1(0)
                for j in range(GROUP):
                    attention_sums(1, 1, 0, j)
                masked_sums(1, 1)
                probs_max(1)
                hT_lo(0)
                steps(e, body, new_layer, peel_layer_end=True, peel_last_layer=True)
                final_sum(T // 2, 0)
                final_statistics(T // 2, 0)


def kernel(**inputs):
    import numpy as np
    import concourse.bacc as bacc
    from concourse.bass_utils import run_bass_kernel_spmd

    nc = bacc.Bacc("TRN2", target_bir_lowering=False, num_devices=1)
    names = ["x", "adj", "L0_gnn_Wq", "L0_gnn_Wk", "L0_gnn_Wv", "L0_gnn_Wo", "L1_gnn_attn_w", "L1_gnn_attn_b",
             "L1_gnn_W1", "L1_gnn_b1", "L1_gnn_W2", "L1_gnn_b2", "L1_gnn_g1", "L1_gnn_beta1", "L1_gnn_g2",
             "L1_gnn_beta2"]
    arrays, args = {}, []
    for name in names:
        a = np.ascontiguousarray(inputs[name])
        arrays[f"in_{name}"] = a
        args.append(nc.dram_tensor(f"in_{name}", a.shape, mybir.dt.from_np(a.dtype), kind="ExternalInput").ap())
    out = nc.dram_tensor("out", arrays["in_x"].shape, F32, kind="ExternalOutput").ap()
    gnn_kernel(nc, *args, out)
    result = run_bass_kernel_spmd(nc, [arrays], core_ids=[0])
    return result.results[0]["out"]
```
